# Optimizing a Trainium2 kernel written in Bass

```python
import numpy as np
import jax
import jax.numpy as jnp

def _softmax(x, axis=-1):
    return jax.nn.softmax(x, axis=axis)

def _gelu(x):
    return jax.nn.gelu(x, approximate=True)

def _silu(x):
    return jax.nn.silu(x)

def _sigmoid(x):
    return jax.nn.sigmoid(x)

def _layernorm(x, axis=-1, eps=1e-05):
    m = jnp.mean(x, axis=axis, keepdims=True)
    v = jnp.var(x, axis=axis, keepdims=True)
    return (x - m) / jnp.sqrt(v + eps)

def _scatter_add(tgt, idx, src, axis=0):
    return tgt.at[idx].add(src)

def _segment_sum(src, seg, n):
    return jax.ops.segment_sum(src, seg, n)
kernel_name = 'mk_xattn_ffn_d1_seqx_r8_8c5fbc'

def setup_inputs(seed: int=0):
    np.random.seed(seed)
    _w = jnp.asarray

    def _rec_inputs():
        import jax
        import jax.numpy as jnp
        _rk = jax.random.key(seed)
        x = -0.0002928 + 1 * jax.random.normal(jax.random.fold_in(_rk, 1), (32, 100, 128), jnp.float32)
        _lenS = 100 - jax.random.randint(jax.random.fold_in(_rk, 7), (32,), 0, max(1, 100 // 4) + 1, jnp.int32)
        _lenS2 = 1444 - jax.random.randint(jax.random.fold_in(_rk, 8), (32,), 0, max(1, 1444 // 4) + 1, jnp.int32)
        _ctx_1024P = jax.random.normal(jax.random.fold_in(_rk, 11), (32, 16, 128), jnp.float32)
        _ctx_1024c = jax.random.dirichlet(jax.random.fold_in(_rk, 511), 0.3 * jnp.ones((16,), jnp.float32), (32, 1444))
        _ctx_1024t = jnp.einsum('bsk,bkd->bsd', _ctx_1024c, _ctx_1024P)
        _ctx_1024t = _ctx_1024t * jax.lax.rsqrt(jnp.mean(jnp.square(_ctx_1024t)) + 1e-12) * 0.953939
        ctx_1024 = -1.39393e-06 + 0.999914 * (_ctx_1024t + 0.3 * jax.random.normal(jax.random.fold_in(_rk, 611), (32, 1444, 128), jnp.float32))
        return (x, ctx_1024)
    x, ctx_1024 = _rec_inputs()

    def _L0_xattn_setup():
        import jax, jax.numpy as jnp
        import numpy as np
        DIM = 128
        HEADS = 16
        HEAD_DIM = DIM // HEADS
        SCALE = HEAD_DIM ** (-0.5)
        key = jax.random.key(seed)
        ks = jax.random.split(key, 7)
        b, n = (2, 256)
        x1 = jax.random.normal(ks[0], (b, n, DIM), dtype=jnp.float32)
        x2 = jax.random.normal(ks[1], (b, n, DIM), dtype=jnp.float32)
        s = DIM ** (-0.5)
        wq = jax.random.normal(ks[2], (DIM, DIM), dtype=jnp.float32) * s
        wk = jax.random.normal(ks[3], (DIM, DIM), dtype=jnp.float32) * s
        wv = jax.random.normal(ks[4], (DIM, DIM), dtype=jnp.float32) * s
        wo = jax.random.normal(ks[5], (DIM, DIM), dtype=jnp.float32) * s
        bo = jax.random.normal(ks[6], (DIM,), dtype=jnp.float32) * 0.01
        return {'x1': x1, 'x2': x2, 'wq': wq, 'wk': wk, 'wv': wv, 'wo': wo, 'bo': bo}
    _L0_xattn_all = _L0_xattn_setup()
    _L0_xattn_in = {k: v for k, v in _L0_xattn_all.items() if k in ('wq', 'wk', 'wv', 'wo', 'bo')}
    del _L0_xattn_all

    def _L0_ffn_setup():
        import jax, jax.numpy as jnp
        import numpy as np
        E = 8
        D = 128
        F = 512
        S, B = (256, 2)
        LN_EPS = 1e-05

        def _moe_forward(input_features, centroids, ln_g, ln_b, W1, b1, W2, b2):
            s, b, d = input_features.shape
            x = jnp.swapaxes(input_features, 0, 1).reshape(-1, d)
            logits = x.astype(jnp.float32) @ centroids.astype(jnp.float32).T
            assign = jnp.argmax(logits, axis=-1)
            onehot = jax.nn.one_hot(assign, E, dtype=x.dtype)
            disp = jnp.einsum('te,td->etd', onehot, x)
            mu = disp.mean(-1, keepdims=True)
            var = disp.var(-1, keepdims=True)
            xn = (disp - mu) * jax.lax.rsqrt(var + LN_EPS)
            xn = xn * ln_g[:, None, :] + ln_b[:, None, :]
            h = jax.nn.relu(jnp.einsum('etd,edf->etf', xn, W1) + b1[:, None, :])
            y = jnp.einsum('etf,efd->etd', h, W2) + b2[:, None, :]
            y = disp + y
            out = jnp.einsum('te,etd->td', onehot, y)
            return jnp.swapaxes(out.reshape(b, s, d), 0, 1)
        key = jax.random.key(seed)
        ks = jax.random.split(key, 8)
        scale_in = 1.0 / np.sqrt(D)
        scale_ff = 1.0 / np.sqrt(F)
        return {'input_features': jax.random.normal(ks[0], (S, B, D), dtype=jnp.float32), 'centroids': jax.random.normal(ks[1], (E, D), dtype=jnp.float32) * scale_in, 'ln_g': jnp.ones((E, D), dtype=jnp.float32), 'ln_b': jnp.zeros((E, D), dtype=jnp.float32), 'W1': jax.random.normal(ks[2], (E, D, F), dtype=jnp.float32) * scale_in, 'b1': jax.random.normal(ks[3], (E, F), dtype=jnp.float32) * 0.01, 'W2': jax.random.normal(ks[4], (E, F, D), dtype=jnp.float32) * scale_ff, 'b2': jax.random.normal(ks[5], (E, D), dtype=jnp.float32) * 0.01}
    _L0_ffn_all = _L0_ffn_setup()
    _L0_ffn_in = {k: v for k, v in _L0_ffn_all.items() if k in ('centroids', 'ln_g', 'ln_b', 'W1', 'b1', 'W2', 'b2')}
    del _L0_ffn_all
    return {'x': x, 'ctx_1024': ctx_1024, 'L0_xattn_wq': _L0_xattn_in['wq'], 'L0_xattn_wk': _L0_xattn_in['wk'], 'L0_xattn_wv': _L0_xattn_in['wv'], 'L0_xattn_wo': _L0_xattn_in['wo'], 'L0_xattn_bo': _L0_xattn_in['bo'], 'L0_ffn_centroids': _L0_ffn_in['centroids'], 'L0_ffn_ln_g': _L0_ffn_in['ln_g'], 'L0_ffn_ln_b': _L0_ffn_in['ln_b'], 'L0_ffn_W1': _L0_ffn_in['W1'], 'L0_ffn_b1': _L0_ffn_in['b1'], 'L0_ffn_W2': _L0_ffn_in['W2'], 'L0_ffn_b2': _L0_ffn_in['b2']}

def reference(x, ctx_1024, L0_xattn_wq, L0_xattn_wk, L0_xattn_wv, L0_xattn_wo, L0_xattn_bo, L0_ffn_centroids, L0_ffn_ln_g, L0_ffn_ln_b, L0_ffn_W1, L0_ffn_b1, L0_ffn_W2, L0_ffn_b2):
    import jax
    import jax.numpy as jnp

    def _L0_xattn_ref(x1, x2, wq, wk, wv, wo, bo):
        import jax, jax.numpy as jnp
        import numpy as np
        DIM = 128
        HEADS = 16
        HEAD_DIM = DIM // HEADS
        SCALE = HEAD_DIM ** (-0.5)
        b, n, _ = x1.shape
        m = x2.shape[1]
        q = (x1 @ wq.T).reshape(b, n, HEADS, HEAD_DIM).transpose(0, 2, 1, 3)
        k = (x2 @ wk.T).reshape(b, m, HEADS, HEAD_DIM).transpose(0, 2, 1, 3)
        v = (x2 @ wv.T).reshape(b, m, HEADS, HEAD_DIM).transpose(0, 2, 1, 3)
        dots = jnp.einsum('bhnd,bhmd->bhnm', q, k) * SCALE
        attn = jax.nn.softmax(dots, axis=-1)
        out = jnp.einsum('bhnm,bhmd->bhnd', attn, v)
        out = out.transpose(0, 2, 1, 3).reshape(b, n, DIM)
        return out @ wo.T + bo

    def _L0_ffn_ref(input_features, centroids, ln_g, ln_b, W1, b1, W2, b2):
        import jax, jax.numpy as jnp
        import numpy as np
        E = 8
        D = 128
        F = 512
        S, B = (256, 2)
        LN_EPS = 1e-05

        def _moe_forward(input_features, centroids, ln_g, ln_b, W1, b1, W2, b2):
            s, b, d = input_features.shape
            x = jnp.swapaxes(input_features, 0, 1).reshape(-1, d)
            logits = x.astype(jnp.float32) @ centroids.astype(jnp.float32).T
            assign = jnp.argmax(logits, axis=-1)
            onehot = jax.nn.one_hot(assign, E, dtype=x.dtype)
            disp = jnp.einsum('te,td->etd', onehot, x)
            mu = disp.mean(-1, keepdims=True)
            var = disp.var(-1, keepdims=True)
            xn = (disp - mu) * jax.lax.rsqrt(var + LN_EPS)
            xn = xn * ln_g[:, None, :] + ln_b[:, None, :]
            h = jax.nn.relu(jnp.einsum('etd,edf->etf', xn, W1) + b1[:, None, :])
            y = jnp.einsum('etf,efd->etd', h, W2) + b2[:, None, :]
            y = disp + y
            out = jnp.einsum('te,etd->td', onehot, y)
            return jnp.swapaxes(out.reshape(b, s, d), 0, 1)
        return _moe_forward(input_features, centroids, ln_g, ln_b, W1, b1, W2, b2)
    x = x + _L0_xattn_ref(_layernorm(x, axis=-1), ctx_1024, L0_xattn_wq, L0_xattn_wk, L0_xattn_wv, L0_xattn_wo, L0_xattn_bo)
    x = x + _L0_ffn_ref(_layernorm(x, axis=-1), L0_ffn_centroids, L0_ffn_ln_g, L0_ffn_ln_b, L0_ffn_W1, L0_ffn_b1, L0_ffn_W2, L0_ffn_b2)
    return x

_drawn_inputs = setup_inputs


def setup_inputs(seed=0):
    import zlib

    import numpy as np

    out = dict(_drawn_inputs(seed))
    spreads = {'L0_ffn_ln_g': (1.0, 0.2), 'L0_ffn_ln_b': (0.0, 0.1)}
    factors = {'L0_ffn_b1': 8.0, 'L0_ffn_b2': 8.0}
    for name, (base, spread) in spreads.items():
        noise = np.random.default_rng([zlib.crc32(name.encode()), seed]).standard_normal(out[name].shape)
        drawn = base * np.exp(spread * noise) if base else spread * noise
        out[name] = jnp.asarray(drawn.astype(out[name].dtype))
    for name, factor in factors.items():
        out[name] = (out[name] * factor).astype(out[name].dtype)
    return out
```

```python
from contextlib import ExitStack

import concourse.bass as bass
from concourse import mybir

F32 = mybir.dt.float32
BF16 = mybir.dt.bfloat16
I32 = mybir.dt.int32
ALU = mybir.AluOpType
ACT = mybir.ActivationFunctionType
AX = mybir.AxisListType

B, N, D = 32, 100, 128
M = 1444
H, HD = 16, 8
P = 128
E, F = 8, 512
FC = F // P
KT = -(-M // P)
MPAD = KT * P
LAST = M - (KT - 1) * P
SCALE = float(HD) ** -0.5
EPS = 1e-5
GB = 4
G = B // GB
GT = GB * N
KCH = [(0, 482), (482, 482), (964, 480)]
VCH = 4
HP = H // 2
VW = 2 * HD + 1
UNITS = 16
UB = 3
TERMS = [(0, 0), (0, 1), (0, 2), (1, 0), (1, 1), (2, 0)]
ROWS = len(TERMS) * 2 * HD
JOBS = 6
AHEAD = 2
PSLOTS = 4
THRESHOLD = 60.0
KV_BANK, O_BANK = 7, 6


ARENA = 28800


def build(nc, x, ctxT, wqT, wkT, wvT, woT, bo, centT, lng, lnb, w1, b1, w2, b2, ident, rank, headmask, wox, out):
    with ExitStack() as stack:
        def sb(name, shape, dt=F32):
            return stack.enter_context(nc.sbuf_tensor(name, shape, dt))

        def sem(name):
            return stack.enter_context(nc.semaphore(name))

        ps = stack.enter_context(nc.psum_tensor("ps", [P, 8, 512], F32))

        wq_s, wk_s, wv_s, wo_s = (sb(n, [D, D]) for n in ("wq_s", "wk_s", "wv_s", "wo_s"))
        bo_s = sb("bo_s", [N, D])
        wox_s = sb("wox_s", [P, 4, D])
        cent_s = sb("cent_s", [D, E])
        lng_s, lnb_s = sb("lng_s", [D, E]), sb("lnb_s", [D, E])
        w1_s = sb("w1_s", [D, E, F])
        b1_s = sb("b1_s", [P, E, FC])
        w2_s = sb("w2_s", [P, E, FC, D])
        b2_s = sb("b2_s", [1, E, D])
        ident_s = sb("ident_s", [P, P])
        rank_s = sb("rank_s", [N, E])
        ones_s = sb("ones_s", [1, N])
        headmask_s = sb("headmask_s", [D, H])
        x_s = sb("x_s", [N, B, D])
        qT = sb("qT", [D, B * N])
        qmax, kmax, bound = sb("qmax", [D, B]), sb("kmax", [D, B]), sb("bound", [D, B])
        bmax, brow, btop, bok = sb("bmax", [B, 1]), sb("brow", [1, B]), sb("btop", [1, 1]), sb("bok", [1, 1])
        flag = sb("flag", [1, 1], I32)
        credit = sb("credit", [1, 8])
        ln_sum, ln_mean, ln_ss, ln_var, ln_std, ln_rstd = (
            sb(n, [N, GB]) for n in ("ln_sum", "ln_mean", "ln_ss", "ln_var", "ln_std", "ln_rstd"))

        arena = sb("arena", [P, ARENA])

        class Carver:
            def __init__(self):
                self.at = 0

            def __call__(self, shape, dt=F32):
                n = 1
                for k in shape[1:]:
                    n *= k
                words = n if dt == F32 else -(-n // 2)
                assert self.at + words <= ARENA
                ap = arena[0:shape[0], self.at:self.at + words]
                self.at += words
                if dt != F32:
                    ap = ap.bitcast(dt)
                names = "abcde"[:len(shape) - 1]
                if len(names) > 1:
                    ap = ap.rearrange(f"p ({' '.join(names)}) -> p {' '.join(names)}",
                                      **{k: v for k, v in zip(names, shape[1:])})
                return ap

        cut = Carver()
        ks = [cut([ROWS, HP, MPAD], BF16) for _ in range(2)]
        qs = [cut([ROWS, HP, 2 * N], BF16) for _ in range(2)]
        kparts = cut([D, 3, M], BF16)
        krest = cut([D, KCH[0][1]])
        ctx_s = [cut([D, M]) for _ in range(2)]
        va = [cut([P, KT, HP, VW]) for _ in range(2)]
        after_values = cut.at
        probs = [cut([P, UB, 4 * N]) for _ in range(PSLOTS)]
        o_raw, o_sum, o_norm = cut([P, 4 * N]), cut([P, 4 * N]), cut([P, 4 * N])
        cut = Carver()
        cut.at = after_values
        ln_cen, ln_sq, ln_out = (cut([N, GB, D]) for _ in range(3))
        lnT, qrest, qparts = cut([D, GT]), cut([D, GT]), cut([D, 3, GT], BF16)
        cut = Carver()
        g_ctx, g_kT, g_v, g_qbd = cut([D, M]), cut([D, M]), cut([P, KT, D]), cut([D, H, N])
        g_p, g_pT = cut([N, M]), cut([P, KT, N])
        smax, nbias, ssum, sinv = (cut([N, H]) for _ in range(4))
        g_o, g_oT = cut([N, D]), cut([D, N])
        cut = Carver()
        f_cen, f_sq, f_out, f_out2 = (cut([N, GB, D]) for _ in range(4))
        f_lnT, f_lnT2 = cut([D, GT]), cut([D, GT])
        lmax, lfirst = cut([N, GB]), cut([N, GB])
        leq, lrank, onehot = (cut([N, GB, E]) for _ in range(3))
        xe = cut([D, 2, GT])
        h_s = cut([P, 2, FC, GT])
        acc = cut([N, GB, D])

        k_dram = [nc.dram_tensor(f"k_dram{i}", (3, D, M), BF16).ap() for i in range(2)]
        q_dram = nc.dram_tensor("q_dram", (3, D, B * N), BF16).ap()

        loads = [sem(f"load{i}") for i in range(17)]
        consts_ready = sem("consts_ready")

        block = stack.enter_context(nc.Block())

        def sems(names):
            return [sem(n) for n in names.split()]

        pads_done, zeroed, q_var, q_std, q_norm, q_lnT_ps, q_lnT, q_ps, q_done, q_chain, q_split, q_stored = sems(
            "pads_done zeroed q_var q_std q_norm q_lnT_ps q_lnT q_ps q_done q_chain q_split q_stored")
        ctx_loaded, ks_loaded, qs_loaded = (sems(f"{n}0 {n}1") for n in ("ctx_loaded", "ks_loaded", "qs_loaded"))
        kv_ps, kv_free, v_part, k_steps, k_split, k_stored, sc_ps, exp_done, pv_done = sems(
            "kv_ps kv_free v_part k_steps k_split k_stored sc_ps exp_done pv_done")
        o_copied, o_steps, o_ready, y_ps, y_done, kmax_done = sems("o_copied o_steps o_ready y_ps y_done kmax_done")
        b_chain, b_ps, b_col, flag_ready = sems("b_chain b_ps b_col flag_ready")
        g_x, g_ctx_loaded, g_k_ps, g_k_done, g_v_ps, g_v_done, g_qbd_done = sems(
            "g_x g_ctx_loaded g_k_ps g_k_done g_v_ps g_v_done g_qbd_done")
        g_s_ps, g_bias, g_exp, g_pt_ps, g_pt_done, g_o_ps, g_o_done, g_ot_ps, g_ot_done, g_y_ps, g_chain = sems(
            "g_s_ps g_bias g_exp g_pt_ps g_pt_done g_o_ps g_o_done g_ot_ps g_ot_done g_y_ps g_chain")
        f_var, f_std, f_norm, f_T_ps, f_T, f_lg_ps, f_xe, f_h_ps, f_h, f_y_ps, f_y, f_chain, f_stored = sems(
            "f_var f_std f_norm f_T_ps f_T f_lg_ps f_xe f_h_ps f_h f_y_ps f_y f_chain f_stored")

        def wide(t):
            return t[:, :].unsqueeze(2).to_broadcast([N, GB, D])

        class Chain:
            def __init__(self, eng, s, i, per):
                self.eng, self.s, self.i, self.per, self.n = eng, s, i, per, 0

            def __call__(self, ins):
                self.n += 1
                ins.then_inc(self.s, 1)
                self.eng.wait_ge(self.s, self.i * self.per + self.n)

        def normalise(dve, link, src, dst, cen, sq, var_ready, std_ready, value):
            link(nc.vector.tensor_reduce(ln_sum[:, :], src, AX.X, ALU.add))
            link(nc.vector.tensor_scalar(ln_mean[:, :], ln_sum[:, :], 1.0 / D, None, ALU.mult))
            link(nc.vector.tensor_tensor(cen, src, wide(ln_mean), ALU.subtract))
            link(nc.vector.tensor_tensor(sq, cen, cen, ALU.mult))
            link(nc.vector.tensor_reduce(ln_ss[:, :], sq, AX.X, ALU.add))
            nc.vector.tensor_scalar(ln_var[:, :], ln_ss[:, :], 1.0 / D, EPS, ALU.mult, ALU.add).then_inc(var_ready, 1)
            dve.wait_ge(std_ready, value)
            link(nc.vector.reciprocal(ln_rstd[:, :], ln_std[:, :]))
            return nc.vector.tensor_tensor(dst, cen, wide(ln_rstd), ALU.mult)

        @block.gpsimd
        def _(pool):
            for k in range(2):
                nc.gpsimd.memset(qs[k], 0.0).then_inc(pads_done, 1)
                nc.gpsimd.memset(ks[k][:, :, M:MPAD], 0.0).then_inc(pads_done, 1)
                nc.gpsimd.memset(va[k][:, 0:KT - 1, :, VW - 1:VW], 1.0).then_inc(pads_done, 1)
                nc.gpsimd.memset(va[k][:, KT - 1, :, :], 0.0).then_inc(zeroed, 1)
                pool.wait_ge(zeroed, k + 1)
                nc.gpsimd.memset(va[k][0:LAST, KT - 1, :, VW - 1:VW], 1.0).then_inc(pads_done, 1)

        @block.sync
        def _(sp):
            pairs = [(x_s[:, :, :], x.rearrange("b n d -> n b d")), (wq_s[:, :], wqT), (ident_s[:, :], ident),
                     (wk_s[:, :], wkT), (wv_s[:, :], wvT), (wo_s[:, :], woT),
                     (bo_s[:, :], bo), (cent_s[:, :], centT), (lng_s[:, :], lng), (lnb_s[:, :], lnb),
                     (w1_s[:, :, :], w1), (b1_s[:, :, :], b1), (w2_s[:, :, :, :], w2), (b2_s[:, :, :], b2),
                     (rank_s[:, :], rank), (headmask_s[:, :], headmask), (wox_s[:, :, :], wox)]
            for k in (0, 1, 2, 6, 3, 4):
                sp.dma_start(*pairs[k]).then_inc(loads[k], 16)
            for k in range(2):
                sp.dma_start(ctx_s[k], ctxT[k]).then_inc(ctx_loaded[k], 16)
            for k in (5, 7, 8, 9, 10, 11, 12, 13, 14, 15, 16):
                sp.dma_start(*pairs[k]).then_inc(loads[k], 16)
            with sp.Fori(0, G) as g:
                sp.wait_ge(q_split, g + 1)
                sp.dma_start(q_dram[:, :, bass.ds(g * GT, GT)].rearrange("t d n -> d t n"), qparts).then_inc(q_stored, 16)
            sp.wait_ge(q_stored, (G + 1) * 16)
            sp.wait_ge(pads_done, 8)

            def operands(kb, half, par, next_ctx, recycled):
                if next_ctx:
                    sp.wait_ge(kv_ps, kb * JOBS)
                    sp.dma_start(ctx_s[1 - par], ctxT[bass.ds(kb + 1, 1)].squeeze(0)).then_inc(ctx_loaded[1 - par], 16)
                if recycled:
                    sp.wait_ge(sc_ps, (kb - 1) * UNITS)
                for t, (_, part) in enumerate(TERMS):
                    src = q_dram[part, :, bass.ds(kb * N, N)].rearrange("(p s d) n -> s d p n", p=HP, s=2)
                    for s in range(2):
                        r = (2 * t + s) * HD
                        sp.dma_start(qs[par][r:r + HD, :, s * N:(s + 1) * N], src[s]).then_inc(qs_loaded[par], 16)
                sp.wait_ge(k_split, (kb + 1) * 3)
                sp.dma_start(k_dram[par].rearrange("t d m -> d t m"), kparts).then_inc(k_stored, 16)
                sp.wait_ge(k_stored, (kb + 1) * 16)
                for t, (part, _) in enumerate(TERMS):
                    src = k_dram[par][part].rearrange("(p r) m -> r p m", p=HP)
                    sp.dma_start(ks[par][2 * t * HD:2 * (t + 1) * HD, :, 0:M], src).then_inc(ks_loaded[par], 16)

            operands(0, 0, 0, False, False)
            operands(1, 0, 1, True, False)
            with sp.Fori(0, B // 2 - 2) as i:
                operands(i * 2 + 2, i + 1, 0, True, True)
                operands(i * 2 + 3, i + 1, 1, True, True)
            operands(B - 2, B // 2 - 1, 0, True, True)
            operands(B - 1, B // 2 - 1, 1, False, True)

            sp.wait_ge(flag_ready, 1)
            unbounded = sp.value_load(flag[0:1, 0:1], min_val=0, max_val=1)
            with sp.If(unbounded):
                sp.dma_start(*pairs[0]).then_inc(g_x, 16)
                with sp.Fori(0, B) as b:
                    sp.wait_ge(g_v_ps, b + 1)
                    sp.dma_start(g_ctx, ctxT[b]).then_inc(g_ctx_loaded, 16)
            with sp.Fori(0, G) as g:
                sp.wait_ge(f_y, (g * E + E) * GB)
                sp.dma_start(out[bass.ds(g * GB, GB)].rearrange("b n d -> n b d"), acc).then_inc(f_stored, 16)
            sp.wait_ge(f_stored, (G + 1) * 16)

        @block.scalar
        def _(act):
            with act.Fori(0, G) as g:
                act.wait_ge(q_var, g + 1)
                nc.scalar.activation(ln_std[:, :], ln_var[:, :], ACT.Sqrt).then_inc(q_std, 1)
                act.wait_ge(q_ps, g + 1)
                nc.scalar.activation(qT[:, bass.ds(g * GT, GT)], ps[:, 1, 0:GT], ACT.Copy).then_inc(q_done, 1)
            with act.Fori(0, B) as b:
                for u in range(UNITS):
                    act.wait_ge(sc_ps, b * UNITS + u + 1)
                    act.wait_ge(pv_done, b * UNITS + u + 1)
                    r = UB * (u % 2)
                    nc.scalar.activation(probs[u % PSLOTS], ps[:, r:r + UB, 0:4 * N], ACT.Exp, scale=SCALE)\
                        .then_inc(exp_done, 1)

            act.wait_ge(flag_ready, 1)
            unbounded = act.value_load(flag[0:1, 0:1], min_val=0, max_val=1)
            with act.If(unbounded):
                with act.Fori(0, B) as b:
                    for h in range(H):
                        act.wait_ge(g_bias, b * H + h + 1)
                        if h:
                            act.wait_ge(g_pt_ps, b * H + h)
                        nc.scalar.activation(g_p.rearrange("n (c m) -> n c m", c=4),
                                             ps[0:N, 0:4, 0:M // 4], ACT.Exp, bias=nbias[:, h:h + 1],
                                             scale=SCALE, accum_out=ssum[:, h:h + 1]).then_inc(g_exp, 1)
            with act.Fori(0, G) as g:
                for k in range(2):
                    act.wait_ge(f_var, g * 2 + k + 1)
                    nc.scalar.activation(ln_std[:, :], ln_var[:, :], ACT.Sqrt).then_inc(f_std, 1)
                for e in range(E):
                    for c in range(FC):
                        act.wait_ge(f_h_ps, g * E * FC + e * FC + c + 1)
                        if c == 0 and e >= 2:
                            act.wait_ge(f_y_ps, g * E + e - 1)
                        nc.scalar.activation(h_s[:, e % 2, c, :], ps[:, 4 + c, 0:GT], ACT.Relu,
                                             bias=b1_s[:, e, c:c + 1]).then_inc(f_h, 1)

        @block.vector
        def _(dve):
            nc.vector.memset(ones_s[:, :], 1.0).then_inc(consts_ready, 1)
            nc.vector.memset(ps[:, O_BANK, :], 0.0).then_inc(o_copied, 1)
            nc.vector.memset(credit[0:1, 0:1], 0.0).then_inc(pv_done, PSLOTS)
            nc.vector.memset(credit[0:1, 1:2], 0.0).then_inc(q_stored, 16)
            nc.vector.memset(credit[0:1, 2:3], 0.0).then_inc(y_done, 1)
            nc.vector.memset(credit[0:1, 6:7], 0.0).then_inc(o_ready, 1)
            nc.vector.memset(credit[0:1, 3:4], 0.0).then_inc(y_ps, 1)
            nc.vector.memset(credit[0:1, 4:5], 0.0).then_inc(g_v_ps, 1)
            nc.vector.memset(credit[0:1, 5:6], 0.0).then_inc(f_stored, 16)
            for k in (0, 6):
                dve.wait_ge(loads[k], 16)
            with dve.Fori(0, G) as g:
                link = Chain(dve, q_chain, g, 6 + 5)
                xg = x_s[:, bass.ds(g * GB, GB), :]
                normalise(dve, link, xg, ln_out, ln_cen, ln_sq, q_var, q_std, g + 1).then_inc(q_norm, 1)
                link(nc.vector.tensor_tensor(xg, xg, bo_s[:, :].unsqueeze(1).to_broadcast([N, GB, D]), ALU.add))
                dve.wait_ge(q_lnT_ps, g + 1)
                nc.vector.tensor_copy(lnT, ps[:, 0, 0:GT]).then_inc(q_lnT, 1)
                dve.wait_ge(q_done, g + 1)
                dve.wait_ge(q_stored, g * 16 + 16)
                qg = qT[:, bass.ds(g * GT, GT)]
                link(nc.vector.tensor_copy(qparts[:, 0, :], qg))
                link(nc.vector.tensor_tensor(qrest, qg, qparts[:, 0, :], ALU.subtract))
                link(nc.vector.tensor_copy(qparts[:, 1, :], qrest))
                nc.vector.tensor_tensor(qparts[:, 2, :], qrest, qparts[:, 1, :], ALU.subtract).then_inc(q_split, 1)
                link(nc.vector.tensor_reduce(qmax[:, bass.ds(g * GB, GB)], qg.rearrange("d (b n) -> d b n", b=GB),
                                             AX.X, ALU.max, apply_absolute_value=True))
            dve.wait_ge(pads_done, 8)

            def project(kb, par, j, first):
                dve.wait_ge(kv_ps, kb * JOBS + j + 1)
                if j < 3:
                    m0, mn = KCH[j]
                    if j == 0 and not first:
                        dve.wait_ge(k_stored, kb * 16)
                        dve.wait_ge(kmax_done, kb)
                    if j or not first:
                        dve.wait_ge(k_split, kb * 3 + j)
                    part = [kparts[:, k, m0:m0 + mn] for k in range(3)]
                    kp = ps[:, KV_BANK, 0:mn]
                    nc.vector.tensor_copy(part[0], kp).then_inc(k_steps, 1)
                    dve.wait_ge(k_steps, kb * 6 + 2 * j + 1)
                    nc.vector.tensor_tensor(krest[:, 0:mn], kp, part[0], ALU.subtract).then_inc(kv_free, 1)
                    dve.wait_ge(kv_free, kb * JOBS + j + 1)
                    nc.vector.tensor_copy(part[1], krest[:, 0:mn]).then_inc(k_steps, 1)
                    dve.wait_ge(k_steps, kb * 6 + 2 * j + 2)
                    nc.vector.tensor_tensor(part[2], krest[:, 0:mn], part[1], ALU.subtract).then_inc(k_split, 1)
                    return
                t0 = (j - 3) * VCH
                whole = VCH if j < JOBS - 1 else VCH - 1
                dst = va[par][:, t0:t0 + whole, :, 0:VW - 1]
                src = ps[:, KV_BANK, 0:whole * D].rearrange("m (t p d) -> m t p d", t=whole, p=HP)
                ins = nc.vector.tensor_copy(dst, src)
                if j < JOBS - 1:
                    ins.then_inc(kv_free, 1)
                else:
                    ins.then_inc(v_part, 1)
                    nc.vector.tensor_copy(va[par][0:LAST, KT - 1, :, 0:VW - 1],
                                          ps[0:LAST, KV_BANK, whole * D:VCH * D].rearrange("m (p d) -> m p d", p=HP))\
                        .then_inc(kv_free, 1)

            def largest_key(kb):
                dve.wait_ge(k_split, (kb + 1) * 3)
                nc.vector.tensor_reduce(kmax[:, bass.ds(kb, 1)], kparts[:, 0, :], AX.X, ALU.max, apply_absolute_value=True).then_inc(kmax_done, 1)

            def copy_out(b):
                dve.wait_ge(pv_done, (b + 1) * UNITS + PSLOTS)
                dve.wait_ge(o_ready, b + 1)
                nc.vector.tensor_copy(o_raw, ps[:, O_BANK, 0:4 * N]).then_inc(o_copied, 1)

            def spread_sums(b):
                dve.wait_ge(pads_done, 8)
                dve.wait_ge(o_copied, b + 2)
                nc.vector.stream_shuffle(o_sum, o_raw, [2 * HD] * 32).then_inc(o_steps, 1)

            def divide(b):
                dve.wait_ge(o_steps, 2 * b + 1)
                nc.vector.reciprocal(o_sum, o_sum).then_inc(o_steps, 1)
                dve.wait_ge(o_steps, 2 * b + 2)
                dve.wait_ge(y_ps, b + 1)
                nc.vector.tensor_tensor(o_norm, o_raw, o_sum, ALU.mult).then_inc(o_ready, 1)

            def residual(b):
                dve.wait_ge(y_ps, b + 2)
                xb = x_s[:, bass.ds(b, 1), :].squeeze(1)
                nc.vector.tensor_tensor(xb, xb, ps[0:N, KV_BANK, 0:D], ALU.add).then_inc(y_done, 1)

            def batch(b, par, first, last):
                if not first:
                    copy_out(b - 1)
                if not last:
                    project(b + 1, 1 - par, 0, False)
                if not first:
                    spread_sums(b - 1)
                if not last:
                    project(b + 1, 1 - par, 1, False)
                    project(b + 1, 1 - par, 2, False)
                if not first:
                    divide(b - 1)
                if not last:
                    for j in range(3, JOBS):
                        project(b + 1, 1 - par, j, False)
                    largest_key(b + 1)
                if not first:
                    residual(b - 1)

            for j in range(JOBS):
                project(0, 0, j, True)
            largest_key(0)
            batch(0, 0, True, False)
            with dve.Fori(0, B // 2 - 1) as i:
                batch(i * 2 + 1, 1, False, False)
                batch(i * 2 + 2, 0, False, False)
            batch(B - 1, 1, False, True)
            copy_out(B - 1)
            spread_sums(B - 1)
            divide(B - 1)
            residual(B - 1)

            link = Chain(dve, b_chain, 0, 4)
            dve.wait_ge(kmax_done, B)
            dve.wait_ge(y_done, B + 1)
            dve.wait_ge(q_chain, G * 11)
            nc.vector.tensor_tensor(bound[:, :], qmax[:, :], kmax[:, :], ALU.mult).then_inc(b_col, 1)
            dve.wait_ge(b_ps, 1)
            nc.vector.tensor_reduce(bmax[:, :], ps[0:B, KV_BANK, 0:H], AX.X, ALU.max).then_inc(b_col, 1)
            dve.wait_ge(b_ps, 2)
            link(nc.vector.tensor_reduce(btop[:, :], ps[0:1, KV_BANK, 0:B], AX.X, ALU.max))
            link(nc.vector.tensor_scalar(bok[:, :], btop[:, :], SCALE, THRESHOLD, ALU.mult, ALU.is_le))
            nc.vector.tensor_scalar(flag[:, :], bok[:, :], -1.0, 1.0, ALU.mult, ALU.add).then_inc(flag_ready, 1)
            dve.wait_ge(flag_ready, 1)
            unbounded = dve.value_load(flag[0:1, 0:1], min_val=0, max_val=1)
            with dve.If(unbounded):
                nc.vector.memset(g_v[:, KT - 1, :], 0.0).then_inc(g_v_done, 1)
                dve.wait_ge(g_x, 16)
                with dve.Fori(0, B) as b:
                    link = Chain(dve, g_chain, b, H + 3)
                    nc.vector.tensor_tensor(g_qbd, qT[:, bass.ds(b * N, N)].unsqueeze(1).to_broadcast([D, H, N]),
                                            headmask_s[:, :].unsqueeze(2).to_broadcast([D, H, N]), ALU.mult)\
                        .then_inc(g_qbd_done, 1)
                    dve.wait_ge(g_k_ps, b + 1)
                    nc.vector.tensor_copy(g_kT[:, 0:964].rearrange("d (c m) -> d c m", c=2), ps[:, 0:2, 0:482])\
                        .then_inc(g_k_done, 1)
                    nc.vector.tensor_copy(g_kT[:, 964:M], ps[:, 2, 0:480]).then_inc(g_k_done, 1)
                    dve.wait_ge(g_v_ps, b + 2)
                    nc.vector.tensor_copy(g_v[:, 0:KT - 1, :].rearrange("p t d -> p (t d)"),
                                          ps[:, 4:7, :].rearrange("p c m -> p (c m)")[:, 0:(KT - 1) * D])\
                        .then_inc(g_v_done, 1)
                    nc.vector.tensor_copy(g_v[0:LAST, KT - 1, :], ps[0:LAST, 6, 3 * D:4 * D]).then_inc(g_v_done, 1)
                    for h in range(H):
                        dve.wait_ge(g_s_ps, b * H + h + 1)
                        link(nc.vector.tensor_reduce(smax[:, h:h + 1], ps[0:N, 0:4, 0:M // 4], AX.XY, ALU.max))
                        nc.vector.tensor_scalar(nbias[:, h:h + 1], smax[:, h:h + 1], -SCALE, None, ALU.mult)\
                            .then_inc(g_bias, 1)
                        dve.wait_ge(g_pt_ps, b * H + h + 1)
                        if h:
                            dve.wait_ge(g_o_ps, b * H + h)
                        nc.vector.tensor_copy(g_pT[:, 0:8, :],
                                              ps[:, 4:6, :].rearrange("p c (t n) -> p (c t) n", t=4)[:, :, 0:N])\
                            .then_inc(g_pt_done, 1)
                        nc.vector.tensor_copy(g_pT[:, 8:11, :],
                                              ps[:, 6, 0:384].rearrange("p (t n) -> p t n", t=3)[:, :, 0:N])\
                            .then_inc(g_pt_done, 1)
                        nc.vector.tensor_copy(g_pT[0:LAST, 11, :], ps[0:LAST, 6, 384:384 + N]).then_inc(g_pt_done, 1)
                    dve.wait_ge(g_exp, b * H + H)
                    link(nc.vector.reciprocal(sinv, ssum))
                    dve.wait_ge(g_o_ps, b * H + H)
                    nc.vector.tensor_tensor(g_o.rearrange("n (h d) -> n h d", h=H),
                                            ps[0:N, 7, 0:D].rearrange("n (h d) -> n h d", h=H),
                                            sinv.unsqueeze(2).to_broadcast([N, H, HD]), ALU.mult).then_inc(g_o_done, 1)
                    dve.wait_ge(g_ot_ps, b + 1)
                    nc.vector.tensor_copy(g_oT, ps[:, 7, 128:128 + N]).then_inc(g_ot_done, 1)
                    xb = x_s[:, bass.ds(b, 1), :].squeeze(1)
                    link(nc.vector.tensor_tensor(xb, xb, bo_s[:, :], ALU.add))
                    dve.wait_ge(g_y_ps, b + 1)
                    link(nc.vector.tensor_tensor(xb, xb, ps[0:N, 7, 256:256 + D], ALU.add))
            for k in (8, 9, 14):
                dve.wait_ge(loads[k], 16)
            with dve.Fori(0, G) as g:
                link = Chain(dve, f_chain, g, 2 * 6 + 1 + 5 + 1)
                xg = x_s[:, bass.ds(g * GB, GB), :]
                link(normalise(dve, link, xg, f_out, f_cen, f_sq, f_var, f_std, g * 2 + 1))
                normalise(dve, link, f_out, f_out2, f_cen, f_sq, f_var, f_std, g * 2 + 2).then_inc(f_norm, 1)
                dve.wait_ge(f_T_ps, g + 1)
                nc.vector.tensor_copy(f_lnT, ps[:, 0, 0:GT]).then_inc(f_T, 1)
                nc.vector.tensor_copy(f_lnT2, ps[:, 1, 0:GT]).then_inc(f_T, 1)
                dve.wait_ge(f_lg_ps, g + 1)
                lg = ps[0:N, 2, 0:GB * E].rearrange("n (t e) -> n t e", e=E)
                ranks = rank_s[:, :].unsqueeze(1).to_broadcast([N, GB, E])
                link(nc.vector.tensor_reduce(lmax, lg, AX.X, ALU.max))
                link(nc.vector.tensor_tensor(leq, lg, lmax.unsqueeze(2).to_broadcast([N, GB, E]), ALU.is_equal))
                link(nc.vector.tensor_tensor(lrank, leq, ranks, ALU.mult))
                link(nc.vector.tensor_reduce(lfirst, lrank, AX.X, ALU.max))
                link(nc.vector.tensor_tensor(onehot, ranks, lfirst.unsqueeze(2).to_broadcast([N, GB, E]), ALU.is_equal))
                dve.wait_ge(f_stored, g * 16 + 16)
                link(nc.vector.tensor_tensor(acc, xg, f_out, ALU.add))

                def expert_input(e):
                    if e >= 2:
                        dve.wait_ge(f_h_ps, g * E * FC + (e - 1) * FC)
                    nc.vector.tensor_scalar(xe[:, e % 2, :], f_lnT2, lng_s[:, e:e + 1], lnb_s[:, e:e + 1],
                                            ALU.mult, ALU.add).then_inc(f_xe, 1)

                dve.wait_ge(f_T, g * 2 + 2)
                expert_input(0)
                for e in range(E):
                    if e + 1 < E:
                        expert_input(e + 1)
                    dve.wait_ge(f_y_ps, g * E + e + 1)
                    if e:
                        dve.wait_ge(f_y, (g * E + e) * GB)
                    for t in range(GB):
                        nc.vector.scalar_tensor_tensor(out=acc[:, t, :], in0=ps[0:N, e % 2, t * D:(t + 1) * D],
                                                       scalar=onehot[:, t, e:e + 1], in1=acc[:, t, :],
                                                       op0=ALU.mult, op1=ALU.add).then_inc(f_y, 1)

        @block.tensor
        def _(pe):
            for k in (1, 2):
                pe.wait_ge(loads[k], 16)
            with pe.Fori(0, G) as g:
                pe.wait_ge(q_norm, g + 1)
                for t in range(GB):
                    last = nc.tensor.transpose(ps[:, 0, t * N:(t + 1) * N], ln_out[:, t, :], ident_s[0:N, 0:N])
                last.then_inc(q_lnT_ps, 1)
                pe.wait_ge(q_lnT, g + 1)
                nc.tensor.matmul(ps[:, 1, 0:GT], wq_s[:, :], lnT, start=True, stop=True).then_inc(q_ps, 1)
            pe.wait_ge(q_done, G)
            for k in (3, 4):
                pe.wait_ge(loads[k], 16)

            def project(kb, half, par, j, shared):
                if j == 0:
                    pe.wait_ge(ctx_loaded[par], (half + 1) * 16)
                    if shared:
                        pe.wait_ge(y_done, kb - 1)
                if shared or kb or j:
                    pe.wait_ge(kv_free, kb * JOBS + j)
                if j < 3:
                    m0, mn = KCH[j]
                    last = nc.tensor.matmul(ps[:, KV_BANK, 0:mn], wk_s[:, :], ctx_s[par][:, m0:m0 + mn],
                                            start=True, stop=True)
                else:
                    for k in range(VCH):
                        t = (j - 3) * VCH + k
                        mn = min(P, M - t * P)
                        last = nc.tensor.matmul(ps[0:mn, KV_BANK, k * D:(k + 1) * D], ctx_s[par][:, t * P:t * P + mn],
                                                wv_s[:, :], start=True, stop=True)
                last.then_inc(kv_ps, 1)

            def scores(b, half, par, u, fresh):
                if u == 0:
                    pe.wait_ge(ks_loaded[par], (half + 1) * len(TERMS) * 16)
                    pe.wait_ge(qs_loaded[par], (half + 1) * 2 * len(TERMS) * 16)
                if not fresh:
                    pe.wait_ge(exp_done, b * UNITS + u - 1)
                for k in range(UB):
                    t, quad = divmod(UB * u + k, 4)
                    for i in range(2):
                        p = 2 * quad + i
                        last = nc.tensor.matmul(ps[:, UB * (u % 2) + k, i * 2 * N:(i + 1) * 2 * N],
                                                ks[par][:, p, t * P:(t + 1) * P], qs[par][:, p, :],
                                                start=True, stop=True)
                last.then_inc(sc_ps, 1)

            def values(b, par, u, alone):
                if alone:
                    pe.wait_ge(exp_done, b * UNITS + u + 1)
                if u == 0:
                    pe.wait_ge(kv_free, (b + 1) * JOBS)
                    pe.wait_ge(v_part, b + 1)
                    pe.wait_ge(o_copied, b + 1)
                for k in range(UB):
                    t, quad = divmod(UB * u + k, 4)
                    for i in range(2):
                        p = 2 * quad + i
                        q, c = 32 * (p % 4), 2 * N * (p // 4)
                        last = nc.tensor.matmul(ps[q:q + VW, O_BANK, c:c + 2 * N], va[par][:, t, p, :],
                                                probs[u % PSLOTS][:, k, i * 2 * N:(i + 1) * 2 * N],
                                                start=(t == 0 and p < 4), stop=(t == KT - 1 and p >= 4),
                                                skip_group_check=True)
                last.then_inc(pv_done, 1)

            def output(b, jobs):
                pe.wait_ge(kv_free, jobs * JOBS)
                pe.wait_ge(o_ready, b + 2)
                for c in range(4):
                    last = nc.tensor.matmul(ps[0:N, KV_BANK, 0:D], o_norm[:, c * N:(c + 1) * N], wox_s[:, c, :],
                                            start=(c == 0), stop=(c == 3))
                last.then_inc(y_ps, 1)

            KV_SLOTS = {0: 0, 2: 1, 4: 2, 6: 3, 8: 4, 10: 5}

            def batch(b, half, par, first, last):
                for u in range(UNITS):
                    v = u + AHEAD
                    if v < UNITS:
                        scores(b, half, par, v, False)
                    elif not last:
                        scores(b + 1, half + par, 1 - par, v - UNITS, False)
                    if not last and u in KV_SLOTS:
                        project(b + 1, half + par, 1 - par, KV_SLOTS[u], not first)
                    if not first and u == 13:
                        output(b - 1, B if last else b + 2)
                    values(b, par, u, last and v >= UNITS)

            for j in range(JOBS):
                project(0, 0, 0, j, False)
            pe.wait_ge(pads_done, 8)
            for k in (16, 15):
                pe.wait_ge(loads[k], 16)
            for u in range(AHEAD):
                scores(0, 0, 0, u, True)
            batch(0, 0, 0, True, False)
            with pe.Fori(0, B // 2 - 1) as i:
                batch(i * 2 + 1, i, 1, False, False)
                batch(i * 2 + 2, i + 1, 0, False, False)
            batch(B - 1, B // 2 - 1, 1, False, True)
            pe.wait_ge(y_done, B)
            output(B - 1, B)

            pe.wait_ge(b_col, 1)
            nc.tensor.matmul(ps[0:B, KV_BANK, 0:H], bound[:, :], headmask_s[:, :], start=True, stop=True).then_inc(b_ps, 1)
            pe.wait_ge(b_col, 2)
            nc.tensor.transpose(ps[0:1, KV_BANK, 0:B], bmax[:, :], ident_s[0:B, 0:B]).then_inc(b_ps, 1)
            pe.wait_ge(flag_ready, 1)
            unbounded = pe.value_load(flag[0:1, 0:1], min_val=0, max_val=1)
            with pe.If(unbounded):
                pe.wait_ge(loads[5], 16)
                with pe.Fori(0, B) as b:
                    pe.wait_ge(g_ctx_loaded, b * 16 + 16)
                    for c, (m0, mn) in enumerate(KCH):
                        last = nc.tensor.matmul(ps[:, c, 0:mn], wk_s[:, :], g_ctx[:, m0:m0 + mn], start=True, stop=True)
                    last.then_inc(g_k_ps, 1)
                    for t in range(KT):
                        mn = min(P, M - t * P)
                        last = nc.tensor.matmul(ps[0:mn, 4 + t // 4, (t % 4) * D:(t % 4 + 1) * D],
                                                g_ctx[:, t * P:t * P + mn], wv_s[:, :], start=True, stop=True)
                    last.then_inc(g_v_ps, 1)
                    pe.wait_ge(g_k_done, b * 2 + 2)
                    pe.wait_ge(g_v_done, b * 2 + 3)
                    pe.wait_ge(g_qbd_done, b + 1)
                    for h in range(H):
                        if h:
                            pe.wait_ge(g_exp, b * H + h)
                        for c in range(4):
                            last = nc.tensor.matmul(ps[0:N, c, 0:M // 4], g_qbd[:, h, :],
                                                    g_kT[:, c * (M // 4):(c + 1) * (M // 4)], start=True, stop=True)
                        last.then_inc(g_s_ps, 1)
                        pe.wait_ge(g_exp, b * H + h + 1)
                        for t in range(KT):
                            mn = min(P, M - t * P)
                            last = nc.tensor.transpose(ps[0:mn, 4 + t // 4, (t % 4) * D:(t % 4) * D + N],
                                                       g_p[:, t * P:t * P + mn], ident_s[0:N, 0:N])
                        last.then_inc(g_pt_ps, 1)
                        pe.wait_ge(g_pt_done, (b * H + h + 1) * 3)
                        for t in range(KT):
                            mn = min(P, M - t * P)
                            last = nc.tensor.matmul(ps[0:N, 7, h * HD:(h + 1) * HD], g_pT[0:mn, t, :],
                                                    g_v[0:mn, t, h * HD:(h + 1) * HD], start=(t == 0), stop=(t == KT - 1))
                        last.then_inc(g_o_ps, 1)
                    pe.wait_ge(g_o_done, b + 1)
                    nc.tensor.transpose(ps[:, 7, 128:128 + N], g_o, ident_s[0:N, 0:N]).then_inc(g_ot_ps, 1)
                    pe.wait_ge(g_ot_done, b + 1)
                    nc.tensor.matmul(ps[0:N, 7, 256:256 + D], g_oT, wo_s[:, :], start=True, stop=True).then_inc(g_y_ps, 1)
                    pe.wait_ge(g_chain, b * (H + 3) + H + 3)
            for k in (7, 10, 11, 12, 13):
                pe.wait_ge(loads[k], 16)
            pe.wait_ge(consts_ready, 1)
            with pe.Fori(0, G) as g:
                pe.wait_ge(f_norm, g + 1)
                for k, src in enumerate((f_out, f_out2)):
                    for t in range(GB):
                        last = nc.tensor.transpose(ps[:, k, t * N:(t + 1) * N], src[:, t, :], ident_s[0:N, 0:N])
                last.then_inc(f_T_ps, 1)
                pe.wait_ge(f_T, g * 2 + 2)
                for t in range(GB):
                    last = nc.tensor.matmul(ps[0:N, 2, t * E:(t + 1) * E], f_lnT[:, t * N:(t + 1) * N], cent_s[:, :],
                                            start=True, stop=True)
                last.then_inc(f_lg_ps, 1)

                def hidden(e):
                    pe.wait_ge(f_xe, g * E + e + 1)
                    for c in range(FC):
                        if e:
                            pe.wait_ge(f_h, g * E * FC + (e - 1) * FC + c + 1)
                        nc.tensor.matmul(ps[:, 4 + c, 0:GT], w1_s[:, e, c * P:(c + 1) * P], xe[:, e % 2, :],
                                         start=True, stop=True).then_inc(f_h_ps, 1)

                def output(e):
                    pe.wait_ge(f_h, g * E * FC + (e + 1) * FC)
                    if e >= 2:
                        pe.wait_ge(f_y, (g * E + e - 1) * GB)
                    for t in range(GB):
                        o = ps[0:N, e % 2, t * D:(t + 1) * D]
                        nc.tensor.matmul(o, ones_s[:, :], b2_s[:, e, :], start=True, stop=False)
                        for c in range(FC):
                            last = nc.tensor.matmul(o, h_s[:, e % 2, c, t * N:(t + 1) * N], w2_s[:, e, c, :],
                                                    start=False, stop=(c == FC - 1))
                    last.then_inc(f_y_ps, 1)

                hidden(0)
                for e in range(E):
                    if e + 1 < E:
                        hidden(e + 1)
                    output(e)
                pe.wait_ge(f_y, (g * E + E) * GB)


def kernel(x, ctx_1024, L0_xattn_wq, L0_xattn_wk, L0_xattn_wv, L0_xattn_wo, L0_xattn_bo, L0_ffn_centroids,
           L0_ffn_ln_g, L0_ffn_ln_b, L0_ffn_W1, L0_ffn_b1, L0_ffn_W2, L0_ffn_b2):
    import numpy as np
    import concourse.bacc as bacc
    from concourse.bass_utils import run_bass_kernel_spmd

    def lay(a):
        return np.ascontiguousarray(np.asarray(a))

    arrays = {
        "x": lay(x),
        "ctxT": lay(np.asarray(ctx_1024).transpose(0, 2, 1)),
        "wqT": lay(np.asarray(L0_xattn_wq).T), "wkT": lay(np.asarray(L0_xattn_wk).T),
        "wvT": lay(np.asarray(L0_xattn_wv).T), "woT": lay(np.asarray(L0_xattn_wo).T),
        "bo": lay(np.broadcast_to(np.asarray(L0_xattn_bo), (N, D))),
        "centT": lay(np.asarray(L0_ffn_centroids).T),
        "lng": lay(np.asarray(L0_ffn_ln_g).T), "lnb": lay(np.asarray(L0_ffn_ln_b).T),
        "w1": lay(np.asarray(L0_ffn_W1).transpose(1, 0, 2)),
        "b1": lay(np.asarray(L0_ffn_b1).reshape(E, FC, P).transpose(2, 0, 1)),
        "w2": lay(np.asarray(L0_ffn_W2).reshape(E, FC, P, D).transpose(2, 0, 1, 3)),
        "b2": lay(np.asarray(L0_ffn_b2).reshape(1, E, D)),
        "ident": np.eye(P, dtype=np.float32),
        "rank": np.broadcast_to(np.arange(E, 0, -1, dtype=np.float32), (N, E)).copy(),
        "headmask": np.kron(np.eye(H, dtype=np.float32), np.ones((HD, 1), np.float32)),
    }
    wo = arrays["woT"].reshape(2, 4, 2, HD, D)
    wox = np.zeros((4, 32, 2, 2, D), np.float32)
    for half in range(2):
        for side in range(2):
            wox[:, side * HD:(side + 1) * HD, half, side, :] = wo[half, :, side]
    arrays["wox"] = wox.reshape(P, 4, D)
    nc = bacc.Bacc("TRN2", target_bir_lowering=False, num_devices=1)
    ins = [nc.dram_tensor(f"in_{n}", a.shape, mybir.dt.from_np(a.dtype), kind="ExternalInput").ap()
           for n, a in arrays.items()]
    out = nc.dram_tensor("out_x", (B, N, D), F32, kind="ExternalOutput").ap()
    build(nc, *ins, out)
    r = run_bass_kernel_spmd(nc, [{f"in_{n}": a for n, a in arrays.items()}], core_ids=[0])
    return r.results[0]["out_x"]
```

```python
from contextlib import ExitStack

import concourse.bass as bass
from concourse import mybir

F32 = mybir.dt.float32
BF16 = mybir.dt.bfloat16
I32 = mybir.dt.int32
ALU = mybir.AluOpType
ACT = mybir.ActivationFunctionType
AX = mybir.AxisListType

B, N, D = 32, 100, 128
M = 1444
H, HD = 16, 8
P = 128
E, F = 8, 512
FC = F // P
KT = -(-M // P)
MPAD = KT * P
LAST = M - (KT - 1) * P
SCALE = float(HD) ** -0.5
EPS = 1e-5
KCH = [(0, 482), (482, 482), (964, 480)]
KC = len(KCH)
VCH = 4
HP = H // 2
VW = 2 * HD + 1
UNITS = 16
UB = 3
TERMS = [(0, 0), (0, 1), (0, 2), (1, 0), (1, 1), (2, 0)]
ROWS = len(TERMS) * 2 * HD
RUNS = [(0, 3), (3, 2), (5, 1)]
AHEAD = 2
PSLOTS = 4
THRESHOLD = 60.0
O_BANK, AUX_BANK = 6, 7

JOBS = ["V0", "V1", "V2", "K0", "K1", "K2", "O", "T", "Q", "R0", "R1", "R2"]
PREPARE = ["K0", "K1", "K2", "T", "Q"]
SLOT = {"V0": 0, "V1": 1, "V2": 2, "K0": 3, "K1": 5, "K2": 7, "O": 8.5, "T": 9.5, "Q": 10.5, "R0": 11.5, "R1": 12.5,
        "R2": 14}
KINDS = {
    "before": [*PREPARE, "V0", "V1", "V2"],
    "before1": PREPARE,
    "first": [n for n in JOBS if n[0] in "VKTQ"],
    "middle": JOBS,
    "late": [n for n in JOBS if n[0] in "VOR"],
    "last": [n for n in JOBS if n[0] in "OR"],
    "after": [n for n in JOBS if n[0] in "OR"],
    "again": ["T", "Q", "O", "R0", "R1", "R2"],
}
FIRST_JOB, BASE = {}, 0
for _kind, _batches in (("before", 1), ("before1", 1), ("first", 1), ("middle", B - 3), ("late", 1), ("last", 1),
                        ("after", 1), ("again", B)):
    FIRST_JOB[_kind], BASE = BASE, BASE + _batches * len(KINDS[_kind])


def job(b, name, kind):
    at = FIRST_JOB[kind] + KINDS[kind].index(name)
    if kind == "middle":
        return (b - 1) * len(JOBS) + at
    if kind == "again":
        return b * len(KINDS[kind]) + at
    return at


ROW = 2 * D + 1
REGION = B * N + P
TILES = (B * N) // P + E - 1
TB = 8
HIDDEN = (2, 6)
PACK = F + FC * D + 6 + D
ARENA = 29700


def build(nc, x, ctxT, wqT, wkT, wvT, woT, wox, bo, centT, pack, ident, rank, headmask, lower, ids, first_row,
          prefix, tile_row, pad_row, out):
    with ExitStack() as stack:
        def sb(name, shape, dt=F32):
            return stack.enter_context(nc.sbuf_tensor(name, shape, dt))

        def sems(names):
            return [stack.enter_context(nc.semaphore(n)) for n in names.split()]

        ps = stack.enter_context(nc.psum_tensor("ps", [P, 8, 512], F32))

        wq_s, wk_s, wv_s, wo_s = (sb(n, [D, D]) for n in ("wq_s", "wk_s", "wv_s", "wo_s"))
        wox_s = sb("wox_s", [P, 4, D])
        bo_s = sb("bo_s", [N, D])
        cent_s = sb("cent_s", [D, E])
        ident_s = sb("ident_s", [P, P])
        rank_s = sb("rank_s", [N, E])
        headmask_s = sb("headmask_s", [D, H])
        lower_s = sb("lower_s", [N, 2, N])
        ids_s = sb("ids_s", [N, B], I32)
        first_s = sb("first_s", [N, E])
        prefix_s = sb("prefix_s", [1, E + 1, E])
        tile_row_s = sb("tile_row_s", [1, TILES])
        pad_s = sb("pad_s", [P, ROW])
        ones_s = sb("ones_s", [1, P])
        half_s, eps_s = sb("half_s", [P, 1]), sb("eps_s", [P, 1])
        credit = sb("credit", [1, 12])
        x_s = sb("x_s", [N, B, D])
        x_stats, x_mv, x_var, x_rstd = (sb(n, [N, w]) for n, w in (("x_stats", 6), ("x_mv", 2), ("x_var", 1), ("x_rstd", 1)))
        xn, xnT = sb("xn", [N, D]), sb("xnT", [D, N])
        qparts, qrest = sb("qparts", [D, 3, N], BF16), sb("qrest", [D, N])
        rows = [sb(f"row{k}", [N, ROW]) for k in range(2)]
        r_stats, r_mv, r_var, r_rstd = (sb(n, [N, w]) for n, w in (("r_stats", 6), ("r_mv", 2), ("r_var", 1), ("r_rstd", 1)))
        yT = sb("yT", [D, N])
        lmax, lfirst, slot_f = (sb(n, [N, 1]) for n in ("lmax", "lfirst", "slot_f"))
        leq, lrank, onehot, place, picked = (sb(n, [N, E]) for n in ("leq", "lrank", "onehot", "place", "picked"))
        slot_i = [sb(f"slot_i{k}", [N, 1], I32) for k in range(2)]
        run = sb("run", [N, E])
        qmax, kmax, bound = sb("qmax", [D, B]), sb("kmax", [D, KC, B]), sb("bound", [D, B])
        kall = sb("kall", [D, B])
        bmax, btop, bok = sb("bmax", [B, 1]), sb("btop", [1, 1]), sb("bok", [1, 1])
        flag = sb("flag", [1, 1], I32)
        t_cnt, t_num = sb("t_cnt", [1, E]), sb("t_num", [1, E])
        t_int = sb("t_int", [1, E], I32)
        t_pre, t_cum, t_off = sb("t_pre", [1, E + 1, E]), sb("t_cum", [1, E + 1]), sb("t_off", [1, E])
        t_ge, t_eq = sb("t_ge", [1, TILES, E]), sb("t_eq", [1, TILES, E])
        t_exp, t_row = sb("t_exp", [1, TILES]), sb("t_row", [1, TILES])
        table = sb("table", [1, 2, TILES], I32)
        t_pad = sb("t_pad", [1, E], I32)
        arena = sb("arena", [P, ARENA])

        class Carver:
            def __init__(self):
                self.at = 0

            def __call__(self, shape, dt=F32):
                n = 1
                for k in shape[1:]:
                    n *= k
                words = n if dt == F32 else -(-n // 2)
                assert self.at + words <= ARENA
                ap = arena[0:shape[0], self.at:self.at + words]
                self.at += words
                if dt != F32:
                    ap = ap.bitcast(dt)
                names = "abcde"[:len(shape) - 1]
                if len(names) > 1:
                    ap = ap.rearrange(f"p ({' '.join(names)}) -> p {' '.join(names)}", **dict(zip(names, shape[1:])))
                return ap

        cut = Carver()
        ks = [cut([ROWS, HP, MPAD], BF16) for _ in range(2)]
        qs = [cut([ROWS, HP, 2 * N], BF16) for _ in range(2)]
        kparts = cut([D, 3, M], BF16)
        krest = [cut([D, KCH[0][1]]) for _ in range(KC)]
        ctx_s = [cut([D, M]) for _ in range(2)]
        va = [cut([P, KT, HP, VW]) for _ in range(2)]
        probs = [cut([P, UB, 4 * N]) for _ in range(PSLOTS)]
        o_raw, o_sum, o_norm = (cut([P, 4 * N]) for _ in range(3))
        cut = Carver()
        g_ctx, g_kT, g_v, g_qbd = cut([D, M]), cut([D, M]), cut([P, KT, D]), cut([D, H, N])
        g_p, g_pT = cut([N, M]), cut([P, KT, N])
        smax, nbias, ssum, sinv = (cut([N, H]) for _ in range(4))
        g_o, g_oT, g_qT = cut([N, D]), cut([D, N]), cut([D, N])
        cut = Carver()
        y_t = [cut([P, ROW]) for _ in range(TB)]
        w_t = [cut([P, PACK]) for _ in range(TB)]
        f_stats, f_mv, f_var, f_rstd = ([cut([P, w]) for _ in range(2)] for w in (6, 2, 1, 1))
        f_n = [cut([P, D]) for _ in range(2)]
        f_x = [cut([D, P]) for _ in range(2)]
        f_h = [cut([P, FC, P]) for _ in range(2)]
        f_o = [cut([P, D]) for _ in range(2)]

        k_dram = [nc.dram_tensor(f"k_dram{i}", (3, D, M), BF16).ap() for i in range(2)]
        QW = HP * 2 * N
        q_dram = [nc.dram_tensor(f"q_dram{i}", ((3 + HP - 1) * 2 * HD, QW), BF16).ap() for i in range(2)]
        y_dram = nc.dram_tensor("y_dram", (E * REGION + P, ROW), F32).ap()

        consts = [("x0", x_s[:, 0:2, :], x[0:2].rearrange("b n d -> n b d")), ("wk", wk_s[:, :], wkT),
                  ("ident", ident_s[:, :], ident), ("wq", wq_s[:, :], wqT), ("bo", bo_s[:, :], bo),
                  ("wv", wv_s[:, :], wvT), ("x1", x_s[:, 2:B, :], x[2:B].rearrange("b n d -> n b d")),
                  ("pad", pad_s[:, :], pad_row), ("wox", wox_s[:, :, :], wox), ("cent", cent_s[:, :], centT), ("rank", rank_s[:, :], rank),
                  ("lower", lower_s[:, :, :], lower), ("ids", ids_s[:, :], ids), ("run", run[:, :], first_row),
                  ("first", first_s[:, :], first_row), ("headmask", headmask_s[:, :], headmask),
                  ("prefix", prefix_s[:, :, :], prefix), ("tile_row", tile_row_s[:, :], tile_row),
                  ("wo", wo_s[:, :], woT)]
        loaded = {name: sem for (name, _, _), sem in zip(consts, sems(" ".join(f"load_{c[0]}" for c in consts)))}

        pads_done, zeroed, consts_ready = sems("pads_done zeroed consts_ready")
        ctx_loaded, ks_loaded, qs_loaded, row_stored = (
            sems(f"{n}0 {n}1") for n in ("ctx_loaded", "ks_loaded", "qs_loaded", "row_stored"))
        aux_ps, aux_free, v_part = sems("aux_ps aux_free v_part")
        x_chain, x_var_in, x_std, x_norm, q_chain, q_split, q_cleared = sems(
            "x_chain x_var_in x_std x_norm q_chain q_split q_cleared")
        q_stored = sems("q_stored0 q_stored1 q_stored2")
        k_steps, k_split, k_stored, kmax_done = sems("k_steps k_split k_stored kmax_done")
        sc_ps, exp_done, pv_done = sems("sc_ps exp_done pv_done")
        o_copied, o_steps, o_ready = sems("o_copied o_steps o_ready")
        r_chain, r_var_in, r_std, r_norm, r_hot, r_slot, r_id, p_chain, rp_chain = sems(
            "r_chain r_var_in r_std r_norm r_hot r_slot r_id p_chain rp_chain")
        b_chain, b_ps, b_col, flag_ready = sems("b_chain b_ps b_col flag_ready")
        g_x, g_ctx_loaded, g_k_ps, g_k_done, g_v_ps, g_v_done, g_qbd_done, g_reset, g_pause = sems(
            "g_x g_ctx_loaded g_k_ps g_k_done g_v_ps g_v_done g_qbd_done g_reset g_pause")
        g_s_ps, g_bias, g_exp, g_pt_ps, g_pt_done, g_o_ps, g_o_done, g_ot_ps, g_ot_done, g_chain = sems(
            "g_s_ps g_bias g_exp g_pt_ps g_pt_done g_o_ps g_o_done g_ot_ps g_ot_done g_chain")
        t_chain, t_ready, pads_stored, rows_done = sems("t_chain t_ready pads_stored rows_done")
        y_loaded, w_loaded = (sems(" ".join(f"{n}{k}" for k in range(TB))) for n in ("y_loaded", "w_loaded"))
        out_stored = sems("out_stored0 out_stored1")
        f_stat, f_var_in, f_fchain, f_std, f_norm, f_T_ps, f_T, f_h_ps, f_hid, f_y_ps, f_half, f_o_done = sems(
            "f_stat f_var_in f_fchain f_std f_norm f_T_ps f_T f_h_ps f_hid f_y_ps f_half f_o_done")

        X_STEPS, R_STEPS, Q_STEPS = 2, 7, 3
        block = stack.enter_context(nc.Block())

        class Chain:
            def __init__(self, eng, s, i, per):
                self.eng, self.s, self.i, self.per, self.n = eng, s, i, per, 0

            def __call__(self, ins):
                self.n += 1
                assert self.n <= self.per
                ins.then_inc(self.s, 1)
                self.eng.wait_ge(self.s, self.i * self.per + self.n)

        @block.gpsimd
        def _(pool):
            for k in range(2):
                nc.gpsimd.memset(va[k][:, 0:KT - 1, :, VW - 1:VW], 1.0).then_inc(pads_done, 1)
                nc.gpsimd.memset(va[k][:, KT - 1, :, :], 0.0).then_inc(zeroed, 1)
                pool.wait_ge(zeroed, k + 1)
                nc.gpsimd.memset(va[k][0:LAST, KT - 1, :, VW - 1:VW], 1.0).then_inc(pads_done, 1)
                nc.gpsimd.memset(ks[k][:, :, M:MPAD], 0.0).then_inc(pads_done, 1)
            pool.wait_ge(consts_ready, 5)

            def met():
                pool.wait_ge(consts_ready, 5)

            def last_part(kb, j):
                m0, mn = KCH[j]
                pool.wait_ge(k_steps, kb * 2 * KC + 2 * j + 2)
                nc.gpsimd.tensor_tensor(kparts[:, 2, m0:m0 + mn], krest[j][:, 0:mn], kparts[:, 1, m0:m0 + mn],
                                        ALU.subtract).then_inc(k_split, 1)

            def query_norm(kb):
                pool.wait_ge(x_var_in, kb + 1)
                nc.gpsimd.tensor_tensor(x_var[:, :], x_mv[:, 1:2], eps_s[0:N, :], ALU.add).then_inc(p_chain, 1)
                pool.wait_ge(p_chain, kb + 1)
                nc.gpsimd.tensor_tensor(x_rstd[:, :], x_var[:, :], half_s[0:N, :], ALU.pow).then_inc(x_std, 1)

            def row_norm(b):
                pool.wait_ge(r_var_in, b + 1)
                nc.gpsimd.tensor_tensor(r_var[:, :], r_mv[:, 1:2], eps_s[0:N, :], ALU.add).then_inc(rp_chain, 1)
                pool.wait_ge(rp_chain, b + 1)
                nc.gpsimd.tensor_tensor(r_rstd[:, :], r_var[:, :], half_s[0:N, :], ALU.pow).then_inc(r_std, 1)

            def store_rows(b, data, par):
                met()
                pool.wait_ge(r_norm, b + 1)
                nc.gpsimd.tensor_copy(rows[par][:, 2 * D:2 * D + 1].bitcast(I32), ids_s[:, bass.ds(data, 1)])\
                    .then_inc(r_id, 1)
                met()
                pool.wait_ge(r_id, b + 1)
                pool.wait_ge(r_slot, b + 1)
                nc.gpsimd.indirect_dma_start(y_dram, bass.IndirectOffsetOnAxis(ap=slot_i[par][:, 0:1], axis=0),
                                             rows[par][:, :], None).then_inc(row_stored[par], 16)

            for name in ("ids", "pad"):
                pool.wait_ge(loaded[name], 16)
            for k in range(2):
                nc.gpsimd.dma_start(y_dram[E * REGION + k * P // 2:E * REGION + (k + 1) * P // 2, :],
                                    pad_s[k * P // 2:(k + 1) * P // 2, :]).then_inc(row_stored[k], 16)

            def prepare(kb):
                last_part(kb, 0)
                last_part(kb, 1)
                query_norm(kb)
                last_part(kb, 2)

            def finish_rows(b, par):
                row_norm(b)
                store_rows(b, b, par)

            prepare(0)
            prepare(1)
            prepare(2)
            with pool.Fori(0, B // 2 - 2) as i:
                prepare(i * 2 + 3)
                finish_rows(i * 2, 0)
                prepare(i * 2 + 4)
                finish_rows(i * 2 + 1, 1)
            prepare(B - 1)
            for b in range(B - 4, B):
                finish_rows(b, b % 2)

            pool.wait_ge(flag_ready, 1)
            unbounded = pool.value_load(flag[0:1, 0:1], min_val=0, max_val=1)
            with pool.If(unbounded):
                with pool.Fori(0, B // 2) as i:
                    for par in range(2):
                        query_norm(i * 2 + (B + par))
                        row_norm(i * 2 + (B + par))
                        store_rows(i * 2 + (B + par), i * 2 + par, par)

            def tile_norm(k, j):
                pool.wait_ge(f_var_in, k + 1)
                nc.gpsimd.tensor_tensor(f_var[j % 2], f_mv[j % 2][:, 1:2], eps_s[:, :], ALU.add).then_inc(f_fchain, 1)
                pool.wait_ge(f_fchain, k + 1)
                nc.gpsimd.tensor_tensor(f_rstd[j % 2], f_var[j % 2], half_s[:, :], ALU.pow).then_inc(f_std, 1)

            def tile_out(k, j):
                pool.wait_ge(f_half, k + 1)
                nc.gpsimd.tensor_tensor(f_o[j % 2], f_o[j % 2], y_t[j][:, D:2 * D], ALU.add).then_inc(f_o_done, 1)
                met()
                pool.wait_ge(f_o_done, k + 1)
                nc.gpsimd.indirect_dma_start(out.rearrange("b n d -> (b n) d"),
                                             bass.IndirectOffsetOnAxis(ap=y_t[j][:, 2 * D:2 * D + 1].bitcast(I32), axis=0),
                                             f_o[j % 2], None, bounds_check=B * N - 1, oob_is_err=False)\
                    .then_inc(out_stored[j % 2], 16)

            for j in range(3):
                tile_norm(j, j)
            with pool.Fori(0, TILES // TB - 1) as i:
                for j in range(TB):
                    tile_norm(i * TB + (j + 3), (j + 3) % TB)
                    tile_out(i * TB + j, j)
            for k in range(TILES - TB, TILES):
                if k + 3 < TILES:
                    tile_norm(k + 3, (k + 3) % TB)
                tile_out(k, k % TB)
            for k in range(2):
                pool.wait_ge(out_stored[k], TILES // 2 * 16)

        @block.sync
        def _(sp):
            for k, (name, dst, src) in enumerate(consts):
                if k == 3:
                    for p in range(2):
                        sp.dma_start(ctx_s[p], ctxT[p]).then_inc(ctx_loaded[p], 16)
                sp.dma_start(dst, src).then_inc(loaded[name], 16)
            sp.wait_ge(pads_done, 6)
            sp.wait_ge(consts_ready, 5)
            more = q_dram[0].shape[0] - ROWS
            for p in range(2):
                sp.dma_start(q_dram[p][0:ROWS, :], qs[p].rearrange("r p n -> r (p n)")).then_inc(q_cleared, 16)
                sp.dma_start(q_dram[p][ROWS:, :], qs[p][0:more].rearrange("r p n -> r (p n)")).then_inc(q_cleared, 16)
            sp.wait_ge(q_cleared, 4 * 16)

            def context(kb, par, jobs_done):
                sp.wait_ge(aux_ps, jobs_done)
                sp.dma_start(ctx_s[par], ctxT[bass.ds(kb, 1)].squeeze(0)).then_inc(ctx_loaded[par], 16)

            def operands(kb, par, recycled):
                sp.wait_ge(k_split, (kb + 1) * KC)
                sp.dma_start(k_dram[par].rearrange("t d m -> d t m"), kparts).then_inc(k_stored, 16)
                sp.wait_ge(q_split, kb + 1)
                for t in range(3):
                    sp.dma_start(bass.AP(q_dram[par].tensor, t * 2 * HD * QW, [[HD * QW + N, H], [QW, HD], [1, N]]),
                                 qparts[:, t, :]).then_inc(q_stored[t], 16)
                sp.wait_ge(k_stored, (kb + 1) * 16)
                for t in range(3):
                    sp.wait_ge(q_stored[t], (kb + 1) * 16)
                if recycled:
                    sp.wait_ge(sc_ps, (kb + 1) * UNITS)
                for t, (part, _) in enumerate(TERMS):
                    src = k_dram[par][part].rearrange("(p r) m -> r p m", p=HP)
                    sp.dma_start(ks[par][2 * t * HD:2 * (t + 1) * HD, :, 0:M], src).then_inc(ks_loaded[par], 16)
                for t0, n in RUNS:
                    sp.dma_start(qs[par][t0 * 2 * HD:(t0 + n) * 2 * HD],
                                 bass.AP(q_dram[par].tensor, 0, [[QW, n * 2 * HD], [2 * HD * QW + 2 * N, HP], [1, 2 * N]]))\
                        .then_inc(qs_loaded[par], 16)

            operands(0, 0, False)
            context(2, 0, job(0, "V2", "before") + 1)
            operands(1, 1, False)
            context(3, 1, job(0, "V2", "first") + 1)
            operands(2, 0, True)
            with sp.Fori(0, B // 2 - 2) as i:
                for p in range(2):
                    b = i * 2 + (p + 1)
                    context(b + 3, p, job(b, "V2", "middle") + 1)
                    operands(b + 2, 1 - p, True)
            operands(B - 1, 1, True)

            sp.wait_ge(flag_ready, 1)
            unbounded = sp.value_load(flag[0:1, 0:1], min_val=0, max_val=1)
            with sp.If(unbounded):
                sp.dma_start(x_s[:, :, :], x.rearrange("b n d -> n b d")).then_inc(g_x, 16)
                with sp.Fori(0, B) as b:
                    sp.wait_ge(g_v_ps, b + 1)
                    sp.dma_start(g_ctx, ctxT[b]).then_inc(g_ctx_loaded, 16)

            sp.wait_ge(t_ready, 1)
            for e in range(E):
                row = sp.value_load(t_pad[0:1, e:e + 1], min_val=e * REGION, max_val=(e + 1) * REGION - P)
                sp.dma_start(y_dram[bass.ds(row, P), :], pad_s[:, :]).then_inc(pads_stored, 16)
            sp.wait_ge(pads_stored, E * 16)
            sp.wait_ge(rows_done, 1)

            def tile(k, j, reused):
                if reused is not None:
                    sp.wait_ge(out_stored[j % 2], reused)
                row = sp.value_load(table[0:1, 1, bass.ds(k, 1)], min_val=0, max_val=E * REGION)
                sp.dma_start(y_t[j], y_dram[bass.ds(row, P), :]).then_inc(y_loaded[j], 16)
                expert = sp.value_load(table[0:1, 0, bass.ds(k, 1)], min_val=0, max_val=E - 1)
                sp.dma_start(w_t[j], pack[bass.ds(expert, 1)].squeeze(0)).then_inc(w_loaded[j], 16)

            for j in range(TB):
                tile(j, j, None)
            with sp.Fori(0, TILES // TB - 1) as i:
                for j in range(TB):
                    tile(i * TB + (TB + j), j, (i * (TB // 2) + j // 2) * 16 + 16)

        @block.scalar
        def _(act):
            def exponentials(b):
                for u in range(UNITS):
                    act.wait_ge(sc_ps, b * UNITS + (u + 1 + 2 * UNITS))
                    act.wait_ge(pv_done, b * UNITS + u + 1)
                    r = UB * (u % 2)
                    nc.scalar.activation(probs[u % PSLOTS], ps[:, r:r + UB, 0:4 * N], ACT.Exp, scale=SCALE)\
                        .then_inc(exp_done, 1)

            exponentials(0)
            with act.Fori(1, B) as b:
                exponentials(b)

            act.wait_ge(flag_ready, 1)
            unbounded = act.value_load(flag[0:1, 0:1], min_val=0, max_val=1)
            with act.If(unbounded):
                with act.Fori(0, B) as b:
                    for h in range(H):
                        act.wait_ge(g_bias, b * H + h + 1)
                        if h:
                            act.wait_ge(g_pt_ps, b * H + h)
                        nc.scalar.activation(g_p.rearrange("n (c m) -> n c m", c=4),
                                             ps[0:N, 0:4, 0:M // 4], ACT.Exp, bias=nbias[:, h:h + 1],
                                             scale=SCALE, accum_out=ssum[:, h:h + 1]).then_inc(g_exp, 1)

            def hidden(k, j, half):
                act.wait_ge(w_loaded[j], half * 16 + 16)
                for c in range(FC):
                    if c % 2 == 0:
                        act.wait_ge(f_h_ps, k * 2 + (c // 2 + 1))
                    if c == 0:
                        act.wait_ge(f_y_ps, k + 1)
                    nc.scalar.activation(f_h[j % 2][:, c, :], ps[:, HIDDEN[j % 2] + c // 2, (c % 2) * P:(c % 2 + 1) * P], ACT.Relu,
                                         bias=w_t[j][:, F + FC * D + 2 + c:F + FC * D + 3 + c]).then_inc(f_hid, 1)

            with act.Fori(0, TILES // TB) as i:
                for j in range(TB):
                    hidden(i * TB + j, j, i)

        @block.vector
        def _(dve):
            nc.vector.memset(half_s[:, :], -0.5).then_inc(consts_ready, 1)
            nc.vector.memset(eps_s[:, :], EPS).then_inc(consts_ready, 1)
            nc.vector.memset(qs[0], 0.0).then_inc(consts_ready, 1)
            nc.vector.memset(qs[1], 0.0).then_inc(consts_ready, 1)
            nc.vector.memset(ones_s[:, :], 1.0).then_inc(consts_ready, 1)
            nc.vector.memset(ps[:, O_BANK, :], 0.0).then_inc(o_copied, 1)
            for k, (s, n) in enumerate([(pv_done, PSLOTS), (sc_ps, 2 * UNITS), (o_ready, 1), (g_v_ps, 1), (f_y_ps, 2),
                                        (g_pause, 1)]):
                nc.vector.memset(credit[0:1, k:k + 1], 0.0).then_inc(s, n)
            for name in ("x0", "bo"):
                dve.wait_ge(loaded[name], 16)

            def query_stats(kb, data):
                link = Chain(dve, x_chain, kb, X_STEPS)
                link(nc.vector.bn_stats(x_stats[:, :], x_s[:, bass.ds(data, 1), :].squeeze(1)))
                return link

            def query_variance():
                nc.vector.bn_aggr(x_mv[:, :], x_stats[:, :]).then_inc(x_var_in, 1)

            def query_norm(kb, data):
                xb = x_s[:, bass.ds(data, 1), :].squeeze(1)
                dve.wait_ge(x_std, kb + 1)
                nc.vector.tensor_scalar(xn[:, :], xb, x_mv[:, 0:1], x_rstd[:, :], ALU.subtract, ALU.mult)\
                    .then_inc(x_norm, 1)

            def add_bias(kb, data, link):
                xb = x_s[:, bass.ds(data, 1), :].squeeze(1)
                dve.wait_ge(x_norm, kb + 1)
                link(nc.vector.tensor_tensor(xb, xb, bo_s[:, :], ALU.add))

            def take_xT(n):
                dve.wait_ge(aux_ps, n + 1)
                nc.vector.tensor_copy(xnT[:, :], ps[:, AUX_BANK, 0:N]).then_inc(aux_free, 1)

            def split_queries(kb, n, first=False):
                link = Chain(dve, q_chain, kb, Q_STEPS)
                qp = ps[:, AUX_BANK, 0:N]
                dve.wait_ge(aux_ps, n + 1)
                if not first:
                    for t in range(3):
                        dve.wait_ge(q_stored[t], kb * 16)
                link(nc.vector.tensor_reduce(qmax[:, bass.ds(kb, 1)], qp, AX.X, ALU.max, apply_absolute_value=True))
                link(nc.vector.tensor_copy(qparts[:, 0, :], qp))
                nc.vector.tensor_tensor(qrest[:, :], qp, qparts[:, 0, :], ALU.subtract).then_inc(aux_free, 1)
                dve.wait_ge(aux_free, n + 1)
                link(nc.vector.tensor_copy(qparts[:, 1, :], qrest[:, :]))
                nc.vector.tensor_tensor(qparts[:, 2, :], qrest[:, :], qparts[:, 1, :], ALU.subtract).then_inc(q_split, 1)

            def split_keys(kb, j, n, first):
                m0, mn = KCH[j]
                kp = ps[:, AUX_BANK, 0:mn]
                dve.wait_ge(aux_ps, n + 1)
                if not first:
                    if j == 0:
                        dve.wait_ge(k_stored, kb * 16)
                        dve.wait_ge(kmax_done, kb * KC)
                nc.vector.tensor_copy(kparts[:, 0, m0:m0 + mn], kp).then_inc(k_steps, 1)
                dve.wait_ge(k_steps, kb * 2 * KC + 2 * j + 1)
                nc.vector.tensor_tensor(krest[j][:, 0:mn], kp, kparts[:, 0, m0:m0 + mn], ALU.subtract)\
                    .then_inc(aux_free, 1)
                dve.wait_ge(aux_free, n + 1)
                nc.vector.tensor_copy(kparts[:, 1, m0:m0 + mn], krest[j][:, 0:mn]).then_inc(k_steps, 1)
                nc.vector.tensor_reduce(kmax[:, j, bass.ds(kb, 1)], kparts[:, 0, m0:m0 + mn], AX.X, ALU.max,
                                        apply_absolute_value=True).then_inc(kmax_done, 1)

            def take_values(kb, par, j, n):
                t0 = j * VCH
                whole = VCH if j < KT // VCH - 1 else VCH - 1
                dve.wait_ge(aux_ps, n + 1)
                ins = nc.vector.tensor_copy(
                    va[par][:, t0:t0 + whole, :, 0:VW - 1],
                    ps[:, AUX_BANK, 0:whole * D].rearrange("m (t p d) -> m t p d", t=whole, p=HP))
                if whole == VCH:
                    ins.then_inc(aux_free, 1)
                else:
                    ins.then_inc(v_part, 1)
                    nc.vector.tensor_copy(va[par][0:LAST, KT - 1, :, 0:VW - 1],
                                          ps[0:LAST, AUX_BANK, whole * D:VCH * D].rearrange("m (p d) -> m p d", p=HP))\
                        .then_inc(aux_free, 1)

            def copy_out(b):
                dve.wait_ge(pv_done, (b + 1) * UNITS + PSLOTS)
                dve.wait_ge(o_ready, b + 1)
                nc.vector.tensor_copy(o_raw, ps[:, O_BANK, 0:4 * N]).then_inc(o_copied, 1)

            def spread_sums(b):
                nc.vector.stream_shuffle(o_sum, o_raw, [2 * HD] * 32).then_inc(o_steps, 1)

            def invert(b, half):
                dve.wait_ge(o_steps, 3 * b + 1)
                cols = slice(half * 2 * N, (half + 1) * 2 * N)
                nc.vector.reciprocal(o_sum[:, cols], o_sum[:, cols]).then_inc(o_steps, 1)

            def divide(b, jobs_done):
                dve.wait_ge(o_steps, 3 * b + 3)
                if jobs_done is not None:
                    dve.wait_ge(aux_ps, jobs_done)
                nc.vector.tensor_tensor(o_norm, o_raw, o_sum, ALU.mult).then_inc(o_ready, 1)

            def residual(b, data, half, par, n):
                link = Chain(dve, r_chain, b, R_STEPS)
                row = rows[par][:, D:2 * D]
                dve.wait_ge(aux_ps, n + 1)
                dve.wait_ge(row_stored[par], half * 16 + 16)
                nc.vector.tensor_tensor(row, x_s[:, bass.ds(data, 1), :].squeeze(1), ps[0:N, AUX_BANK, 0:D], ALU.add)\
                    .then_inc(aux_free, 1)
                dve.wait_ge(aux_free, n + 1)
                link(nc.vector.bn_stats(r_stats[:, :], row))
                return link

            def row_variance():
                nc.vector.bn_aggr(r_mv[:, :], r_stats[:, :]).then_inc(r_var_in, 1)

            def row_norm(b, par):
                dve.wait_ge(r_std, b + 1)
                nc.vector.tensor_scalar(rows[par][:, 0:D], rows[par][:, D:2 * D], r_mv[:, 0:1], r_rstd[:, :],
                                        ALU.subtract, ALU.mult).then_inc(r_norm, 1)

            def take_yT(n):
                dve.wait_ge(aux_ps, n + 1)
                nc.vector.tensor_copy(yT[:, :], ps[:, AUX_BANK, 0:N]).then_inc(aux_free, 1)

            def choose(b, link, n):
                lg = ps[0:N, AUX_BANK, 0:E]
                dve.wait_ge(aux_ps, n + 1)
                link(nc.vector.tensor_reduce(lmax[:, :], lg, AX.X, ALU.max))
                nc.vector.tensor_scalar(leq[:, :], lg, lmax[:, :], None, ALU.is_equal).then_inc(aux_free, 1)
                dve.wait_ge(aux_free, n + 1)
                link(nc.vector.tensor_tensor(lrank[:, :], leq[:, :], rank_s[:, :], ALU.mult))
                link(nc.vector.tensor_reduce(lfirst[:, :], lrank[:, :], AX.X, ALU.max))
                nc.vector.tensor_scalar(onehot[:, :], rank_s[:, :], lfirst[:, :], None, ALU.is_equal).then_inc(r_hot, 1)

            def place_rows(b, par, link, n):
                dve.wait_ge(aux_ps, n + 1)
                link(nc.vector.tensor_tensor(place[:, :], ps[0:N, AUX_BANK, 0:E], run[:, :], ALU.add))
                link(nc.vector.tensor_tensor(picked[:, :], place[:, :], onehot[:, :], ALU.mult))
                link(nc.vector.tensor_reduce(slot_f[:, :], picked[:, :], AX.X, ALU.add))
                nc.vector.tensor_copy(slot_i[par][:, :], slot_f[:, :]).then_inc(r_slot, 1)
                nc.vector.tensor_tensor(run[:, :], run[:, :], ps[0:N, AUX_BANK, E:2 * E], ALU.add).then_inc(aux_free, 1)
                dve.wait_ge(aux_free, n + 1)

            def batch(b, half, par, kind):
                names = KINDS[kind]
                values, keys, previous = "V0" in names, "K0" in names, "O" in names
                other = 1 - par
                if previous:
                    copy_out(b - 1)
                    dve.wait_ge(o_copied, b + 1)
                if values:
                    take_values(b + 1, other, 0, job(b, "V0", kind))
                if previous:
                    spread_sums(b - 1)
                if values:
                    take_values(b + 1, other, 1, job(b, "V1", kind))
                if previous:
                    invert(b - 1, 0)
                if values:
                    take_values(b + 1, other, 2, job(b, "V2", kind))
                if previous:
                    invert(b - 1, 1)
                if keys:
                    split_keys(b + 2, 0, job(b, "K0", kind), False)
                if previous:
                    divide(b - 1, None if values else job(b, "O", kind))
                if keys:
                    xlink = query_stats(b + 2, b + 2)
                    split_keys(b + 2, 1, job(b, "K1", kind), False)
                    query_variance()
                    split_keys(b + 2, 2, job(b, "K2", kind), False)
                    query_norm(b + 2, b + 2)
                    add_bias(b + 2, b + 2, xlink)
                if previous:
                    rlink = residual(b - 1, b - 1, half if par else half - 1, other, job(b, "O", kind))
                if keys:
                    take_xT(job(b, "T", kind))
                if previous:
                    row_variance()
                    row_norm(b - 1, other)
                if keys:
                    split_queries(b + 2, job(b, "Q", kind))
                if previous:
                    take_yT(job(b, "R0", kind))
                    choose(b - 1, rlink, job(b, "R1", kind))
                    place_rows(b - 1, other, rlink, job(b, "R2", kind))

            def prepare(kb, kind):
                link = query_stats(kb, kb)
                for j in range(KC):
                    split_keys(kb, j, job(0, f"K{j}", kind), kb == 0)
                    if j == 0:
                        query_variance()
                query_norm(kb, kb)
                add_bias(kb, kb, link)
                take_xT(job(0, "T", kind))
                split_queries(kb, job(0, "Q", kind), kb == 0)

            prepare(0, "before")
            dve.wait_ge(pads_done, 6)
            for j in range(3):
                take_values(0, 0, j, job(0, f"V{j}", "before"))
            prepare(1, "before1")
            for name in ("x1", "rank", "run"):
                dve.wait_ge(loaded[name], 16)
            batch(0, 0, 0, "first")
            with dve.Fori(0, B // 2 - 2) as i:
                batch(i * 2 + 1, i, 1, "middle")
                batch(i * 2 + 2, i + 1, 0, "middle")
            batch(B - 3, B // 2 - 2, 1, "middle")
            batch(B - 2, B // 2 - 1, 0, "late")
            batch(B - 1, B // 2 - 1, 1, "last")
            copy_out(B - 1)
            dve.wait_ge(o_copied, B + 1)
            spread_sums(B - 1)
            invert(B - 1, 0)
            invert(B - 1, 1)
            divide(B - 1, job(B, "O", "after"))
            rlink = residual(B - 1, B - 1, B // 2 - 1, 1, job(B, "O", "after"))
            row_variance()
            row_norm(B - 1, 1)
            take_yT(job(B, "R0", "after"))
            choose(B - 1, rlink, job(B, "R1", "after"))
            place_rows(B - 1, 1, rlink, job(B, "R2", "after"))

            link = Chain(dve, b_chain, 0, 4)
            link(nc.vector.tensor_tensor(kall[:, :], kmax[:, 0, :], kmax[:, 1, :], ALU.max))
            link(nc.vector.tensor_tensor(kall[:, :], kall[:, :], kmax[:, 2, :], ALU.max))
            nc.vector.tensor_tensor(bound[:, :], qmax[:, :], kall[:, :], ALU.mult).then_inc(b_col, 1)
            dve.wait_ge(b_ps, 1)
            nc.vector.tensor_reduce(bmax[:, :], ps[0:B, AUX_BANK, 0:H], AX.X, ALU.max).then_inc(b_col, 1)
            dve.wait_ge(b_ps, 2)
            link(nc.vector.tensor_reduce(btop[:, :], ps[0:1, AUX_BANK, 0:B], AX.X, ALU.max))
            link(nc.vector.tensor_scalar(bok[:, :], btop[:, :], SCALE, THRESHOLD, ALU.mult, ALU.is_le))
            nc.vector.tensor_scalar(flag[:, :], bok[:, :], -1.0, 1.0, ALU.mult, ALU.add).then_inc(flag_ready, 1)
            dve.wait_ge(flag_ready, 1)
            unbounded = dve.value_load(flag[0:1, 0:1], min_val=0, max_val=1)
            with dve.If(unbounded):
                dve.wait_ge(loaded["first"], 16)
                for k in range(2):
                    dve.wait_ge(row_stored[k], (B // 2 + 1) * 16)
                nc.vector.tensor_copy(run[:, :], first_s[:, :]).then_inc(g_reset, 1)
                dve.wait_ge(g_x, 16)
                dve.wait_ge(g_reset, 1)
                with dve.Fori(0, B // 2) as i:
                    for par in range(2):
                        b = i * 2 + par
                        again = i * 2 + (B + par)
                        qlink = query_stats(again, b)
                        dve.wait_ge(g_k_ps, b + 1)
                        nc.vector.tensor_copy(g_kT[:, 0:964].rearrange("d (c m) -> d c m", c=2), ps[:, 0:2, 0:482])\
                            .then_inc(g_k_done, 1)
                        query_variance()
                        nc.vector.tensor_copy(g_kT[:, 964:M], ps[:, 2, 0:480]).then_inc(g_k_done, 1)
                        query_norm(again, b)
                        add_bias(again, b, qlink)
                        take_xT(job(b, "T", "again"))
                        link = Chain(dve, g_chain, b, H + 2)
                        n = job(b, "Q", "again")
                        dve.wait_ge(aux_ps, n + 1)
                        nc.vector.tensor_copy(g_qT, ps[:, AUX_BANK, 0:N]).then_inc(aux_free, 1)
                        dve.wait_ge(aux_free, n + 1)
                        nc.vector.tensor_tensor(g_qbd, g_qT.unsqueeze(1).to_broadcast([D, H, N]),
                                                headmask_s[:, :].unsqueeze(2).to_broadcast([D, H, N]), ALU.mult)\
                            .then_inc(g_qbd_done, 1)
                        dve.wait_ge(g_v_ps, b + 2)
                        nc.vector.tensor_copy(g_v[:, 0:KT - 1, :].rearrange("p t d -> p (t d)"),
                                              ps[:, 4:7, :].rearrange("p c m -> p (c m)")[:, 0:(KT - 1) * D])\
                            .then_inc(g_v_done, 1)
                        nc.vector.tensor_copy(g_v[0:LAST, KT - 1, :], ps[0:LAST, 6, 3 * D:4 * D]).then_inc(g_v_done, 1)
                        for h in range(H):
                            dve.wait_ge(g_s_ps, b * H + h + 1)
                            link(nc.vector.tensor_reduce(smax[:, h:h + 1], ps[0:N, 0:4, 0:M // 4], AX.XY, ALU.max))
                            nc.vector.tensor_scalar(nbias[:, h:h + 1], smax[:, h:h + 1], -SCALE, None, ALU.mult)\
                                .then_inc(g_bias, 1)
                            dve.wait_ge(g_pt_ps, b * H + h + 1)
                            if h:
                                dve.wait_ge(g_o_ps, b * H + h)
                            nc.vector.tensor_copy(g_pT[:, 0:8, :],
                                                  ps[:, 4:6, :].rearrange("p c (t n) -> p (c t) n", t=4)[:, :, 0:N])\
                                .then_inc(g_pt_done, 1)
                            nc.vector.tensor_copy(g_pT[:, 8:11, :],
                                                  ps[:, 6, 0:384].rearrange("p (t n) -> p t n", t=3)[:, :, 0:N])\
                                .then_inc(g_pt_done, 1)
                            nc.vector.tensor_copy(g_pT[0:LAST, 11, :], ps[0:LAST, 6, 384:384 + N]).then_inc(g_pt_done, 1)
                        dve.wait_ge(g_exp, b * H + H)
                        link(nc.vector.reciprocal(sinv, ssum))
                        dve.wait_ge(g_o_ps, b * H + H)
                        nc.vector.tensor_tensor(g_o.rearrange("n (h d) -> n h d", h=H),
                                                ps[0:N, AUX_BANK, 0:D].rearrange("n (h d) -> n h d", h=H),
                                                sinv.unsqueeze(2).to_broadcast([N, H, HD]), ALU.mult).then_inc(g_o_done, 1)
                        dve.wait_ge(g_ot_ps, b + 1)
                        link(nc.vector.tensor_copy(g_oT, ps[:, AUX_BANK, 128:128 + N]))
                        rlink = residual(again, b, i + B // 2, par, job(b, "O", "again"))
                        dve.wait_ge(g_pause, b + 1)
                        nc.vector.memset(credit[0:1, 10:11], 0.0).then_inc(g_pause, 1)
                        row_variance()
                        row_norm(again, par)
                        take_yT(job(b, "R0", "again"))
                        choose(again, rlink, job(b, "R1", "again"))
                        place_rows(again, par, rlink, job(b, "R2", "again"))
                for k in range(2):
                    dve.wait_ge(row_stored[k], (B + 1) * 16)

            for name in ("first", "prefix", "tile_row", "pad"):
                dve.wait_ge(loaded[name], 16)
            link = Chain(dve, t_chain, 0, 19)
            link(nc.vector.tensor_tensor(t_cnt[:, :], run[0:1, :], first_s[0:1, :], ALU.subtract))
            link(nc.vector.tensor_copy(t_pad[:, :], run[0:1, :]))
            link(nc.vector.tensor_scalar(t_int[:, :], t_cnt[:, :], float(P - 1), None, ALU.add))
            link(nc.vector.tensor_scalar(t_int[:, :], t_int[:, :], 7, None, ALU.logical_shift_right))
            link(nc.vector.tensor_copy(t_num[:, :], t_int[:, :]))
            link(nc.vector.tensor_tensor(t_pre[:, :, :], prefix_s[:, :, :],
                                         t_num[:, :].unsqueeze(1).to_broadcast([1, E + 1, E]), ALU.mult))
            link(nc.vector.tensor_reduce(t_cum[:, :], t_pre[:, :, :], AX.X, ALU.add))
            link(nc.vector.tensor_scalar(t_off[:, :], t_cum[:, 0:E], -float(P), None, ALU.mult))
            link(nc.vector.tensor_tensor(t_off[:, :], t_off[:, :], first_s[0:1, :], ALU.add))
            link(nc.vector.tensor_tensor(t_ge[:, :, :], tile_row_s[:, :].unsqueeze(2).to_broadcast([1, TILES, E]),
                                         t_cum[:, 1:E + 1].unsqueeze(1).to_broadcast([1, TILES, E]), ALU.is_ge))
            link(nc.vector.tensor_reduce(t_exp[:, :], t_ge[:, :, :], AX.X, ALU.add))
            link(nc.vector.tensor_scalar(t_row[:, :], t_exp[:, :], -1.0, float(E), ALU.mult, ALU.add))
            link(nc.vector.tensor_tensor(t_eq[:, :, :], t_row[:, :].unsqueeze(2).to_broadcast([1, TILES, E]),
                                         rank_s[0:1, :].unsqueeze(1).to_broadcast([1, TILES, E]), ALU.is_equal))
            link(nc.vector.tensor_tensor(t_eq[:, :, :], t_eq[:, :, :],
                                         t_off[:, :].unsqueeze(1).to_broadcast([1, TILES, E]), ALU.mult))
            link(nc.vector.tensor_reduce(t_row[:, :], t_eq[:, :, :], AX.X, ALU.add))
            link(nc.vector.tensor_scalar(t_ge[:, :, 0], t_exp[:, :], float(E), float(E * REGION), ALU.is_equal, ALU.mult))
            link(nc.vector.scalar_tensor_tensor(out=t_row[:, :], in0=tile_row_s[:, :], scalar=float(P), in1=t_row[:, :],
                                                op0=ALU.mult, op1=ALU.add))
            link(nc.vector.tensor_tensor(t_row[:, :], t_row[:, :], t_ge[:, :, 0], ALU.add))
            link(nc.vector.tensor_scalar(table[:, 1, :], t_row[:, :], float(E * REGION), None, ALU.min))
            nc.vector.tensor_scalar(table[:, 0, :], t_exp[:, :], float(E - 1), None, ALU.min).then_inc(t_ready, 1)
            for k in range(2):
                dve.wait_ge(row_stored[k], (B // 2 + 1) * 16)
            nc.vector.memset(credit[0:1, 11:12], 0.0).then_inc(rows_done, 1)

            def stats(k, j, half):
                dve.wait_ge(y_loaded[j], half * 16 + 16)
                nc.vector.bn_stats(f_stats[j % 2], y_t[j][:, 0:D]).then_inc(f_stat, 1)
                dve.wait_ge(f_stat, k + 1)

            def variance(j):
                nc.vector.bn_aggr(f_mv[j % 2], f_stats[j % 2]).then_inc(f_var_in, 1)

            def normal(k, j):
                dve.wait_ge(f_std, k + 1)
                nc.vector.tensor_scalar(f_n[j % 2], y_t[j][:, 0:D], f_mv[j % 2][:, 0:1], f_rstd[j % 2],
                                        ALU.subtract, ALU.mult).then_inc(f_norm, 1)

            def affine(k, j, half):
                dve.wait_ge(f_T_ps, k + 1)
                dve.wait_ge(w_loaded[j], half * 16 + 16)
                g0 = F + FC * D
                nc.vector.tensor_scalar(f_x[j % 2], ps[:, j % 2, 0:P], w_t[j][:, g0:g0 + 1], w_t[j][:, g0 + 1:g0 + 2],
                                        ALU.mult, ALU.add).then_inc(f_T, 1)

            def finish(k, j, pair):
                dve.wait_ge(f_y_ps, k + 3)
                if pair is not None:
                    dve.wait_ge(out_stored[j % 2], pair * 16)
                nc.vector.tensor_tensor(f_o[j % 2], y_t[j][:, 0:D], ps[:, 4 + j % 2, 0:D], ALU.add).then_inc(f_half, 1)

            def step(k, j, i, pair):
                stats(k + 3, (j + 3) % TB, i + (j + 3) // TB)
                affine(k + 1, (j + 1) % TB, i + (j + 1) // TB)
                variance((j + 3) % TB)
                normal(k + 2, (j + 2) % TB)
                finish(k, j, pair)

            for j in range(3):
                stats(j, j, 0)
                variance(j)
                if j < 2:
                    normal(j, j)
            affine(0, 0, 0)
            for j in range(TB):
                step(j, j, 0, j // 2 if j >= 2 else None)
            with dve.Fori(1, TILES // TB - 1) as i:
                for j in range(TB):
                    step(i * TB + j, j, i, i * (TB // 2) + j // 2)
            for k in range(TILES - TB, TILES - 3):
                step(k, k % TB, TILES // TB - 1, k // 2)
            for k in range(TILES - 3, TILES):
                if k + 1 < TILES:
                    affine(k + 1, (k + 1) % TB, TILES // TB - 1)
                if k + 2 < TILES:
                    normal(k + 2, (k + 2) % TB)
                finish(k, k % TB, k // 2)

        @block.tensor
        def _(pe):
            for name in ("wk", "ident"):
                pe.wait_ge(loaded[name], 16)

            def keys(j, par, n):
                m0, mn = KCH[j]
                if not isinstance(n, int) or n > 0:
                    pe.wait_ge(aux_free, n)
                nc.tensor.matmul(ps[:, AUX_BANK, 0:mn], wk_s[:, :], ctx_s[par][:, m0:m0 + mn], start=True, stop=True)\
                    .then_inc(aux_ps, 1)

            def xT(kb, n):
                pe.wait_ge(aux_free, n)
                pe.wait_ge(x_norm, kb + 1)
                nc.tensor.transpose(ps[:, AUX_BANK, 0:N], xn[:, :], ident_s[0:N, 0:N]).then_inc(aux_ps, 1)

            def queries(n):
                pe.wait_ge(aux_free, n)
                nc.tensor.matmul(ps[:, AUX_BANK, 0:N], wq_s[:, :], xnT[:, :], start=True, stop=True).then_inc(aux_ps, 1)

            def values(j, par, n):
                pe.wait_ge(aux_free, n)
                for k in range(VCH):
                    t = j * VCH + k
                    mn = min(P, M - t * P)
                    last = nc.tensor.matmul(ps[0:mn, AUX_BANK, k * D:(k + 1) * D], ctx_s[par][:, t * P:t * P + mn],
                                            wv_s[:, :], start=True, stop=True)
                last.then_inc(aux_ps, 1)

            def output(b, n):
                pe.wait_ge(aux_free, n)
                pe.wait_ge(o_ready, b + 2)
                for c in range(4):
                    last = nc.tensor.matmul(ps[0:N, AUX_BANK, 0:D], o_norm[:, c * N:(c + 1) * N], wox_s[:, c, :],
                                            start=(c == 0), stop=(c == 3))
                last.then_inc(aux_ps, 1)

            def rowsT(b, par, n):
                pe.wait_ge(aux_free, n)
                pe.wait_ge(r_norm, b + 1)
                nc.tensor.transpose(ps[:, AUX_BANK, 0:N], rows[par][:, 0:D], ident_s[0:N, 0:N]).then_inc(aux_ps, 1)

            def logits(n):
                pe.wait_ge(aux_free, n)
                nc.tensor.matmul(ps[0:N, AUX_BANK, 0:E], yT[:, :], cent_s[:, :], start=True, stop=True).then_inc(aux_ps, 1)

            def ranks(b, n):
                pe.wait_ge(aux_free, n)
                pe.wait_ge(r_hot, b + 1)
                nc.tensor.matmul(ps[0:N, AUX_BANK, 0:E], lower_s[:, 0, :], onehot[:, :], start=True, stop=True)
                nc.tensor.matmul(ps[0:N, AUX_BANK, E:2 * E], lower_s[:, 1, :], onehot[:, :], start=True, stop=True)\
                    .then_inc(aux_ps, 1)

            def scores(b, half, par, u, fresh):
                if u == 0:
                    pe.wait_ge(ks_loaded[par], (half + 1) * len(TERMS) * 16)
                    pe.wait_ge(qs_loaded[par], (half + 1) * len(RUNS) * 16)
                if not fresh:
                    pe.wait_ge(exp_done, b * UNITS + u - 1)
                for k in range(UB):
                    t, quad = divmod(UB * u + k, 4)
                    for i in range(2):
                        p = 2 * quad + i
                        last = nc.tensor.matmul(ps[:, UB * (u % 2) + k, i * 2 * N:(i + 1) * 2 * N],
                                                ks[par][:, p, t * P:(t + 1) * P], qs[par][:, p, :],
                                                start=True, stop=True)
                last.then_inc(sc_ps, 1)

            def weigh(b, par, u, alone):
                if alone:
                    pe.wait_ge(exp_done, b * UNITS + u + 1)
                if u == 0:
                    pe.wait_ge(v_part, b + 1)
                    pe.wait_ge(o_copied, b + 1)
                for k in range(UB):
                    t, quad = divmod(UB * u + k, 4)
                    for i in range(2):
                        p = 2 * quad + i
                        q, c = 32 * (p % 4), 2 * N * (p // 4)
                        last = nc.tensor.matmul(ps[q:q + VW, O_BANK, c:c + 2 * N], va[par][:, t, p, :],
                                                probs[u % PSLOTS][:, k, i * 2 * N:(i + 1) * 2 * N],
                                                start=(t == 0 and p < 4), stop=(t == KT - 1 and p >= 4),
                                                skip_group_check=True)
                last.then_inc(pv_done, 1)

            def prepare(kb, par, kind):
                for j in range(KC):
                    keys(j, par, job(0, f"K{j}", kind))
                xT(kb, job(0, "T", kind))
                queries(job(0, "Q", kind))

            def batch(b, half, par, kind):
                last = kind == "last"
                other, other_half = 1 - par, half + par

                def beside(slot):
                    for name in KINDS[kind]:
                        if SLOT[name] != slot:
                            continue
                        n = job(b, name, kind)
                        if name == "K0":
                            pe.wait_ge(ctx_loaded[par], (half + 2) * 16)
                        if name[0] == "K":
                            keys(int(name[1]), par, n)
                        elif name == "T":
                            xT(b + 2, n)
                        elif name == "Q":
                            queries(n)
                        elif name[0] == "V":
                            values(int(name[1]), other, n)
                        elif name == "O":
                            output(b - 1, n)
                        elif name == "R0":
                            rowsT(b - 1, other, n)
                        elif name == "R1":
                            logits(n)
                        else:
                            ranks(b - 1, n)

                for u in range(UNITS):
                    v = u + AHEAD
                    if v < UNITS:
                        scores(b, half, par, v, False)
                    elif not last:
                        scores(b + 1, other_half, other, v - UNITS, False)
                    beside(u)
                    weigh(b, par, u, last and v >= UNITS)
                    beside(u + 0.5)

            for name in ("wq", "wv"):
                pe.wait_ge(loaded[name], 16)
            pe.wait_ge(ctx_loaded[0], 16)
            prepare(0, 0, "before")
            for j in range(3):
                values(j, 0, job(0, f"V{j}", "before"))
            pe.wait_ge(ctx_loaded[1], 16)
            prepare(1, 1, "before1")
            pe.wait_ge(pads_done, 6)
            pe.wait_ge(consts_ready, 5)
            for name in ("wox", "cent", "lower", "headmask"):
                pe.wait_ge(loaded[name], 16)
            for u in range(AHEAD):
                scores(0, 0, 0, u, True)
            batch(0, 0, 0, "first")
            with pe.Fori(0, B // 2 - 2) as i:
                batch(i * 2 + 1, i, 1, "middle")
                batch(i * 2 + 2, i + 1, 0, "middle")
            batch(B - 3, B // 2 - 2, 1, "middle")
            batch(B - 2, B // 2 - 1, 0, "late")
            batch(B - 1, B // 2 - 1, 1, "last")
            output(B - 1, job(B, "O", "after"))
            rowsT(B - 1, 1, job(B, "R0", "after"))
            logits(job(B, "R1", "after"))
            ranks(B - 1, job(B, "R2", "after"))

            pe.wait_ge(b_col, 1)
            nc.tensor.matmul(ps[0:B, AUX_BANK, 0:H], bound[:, :], headmask_s[:, :], start=True, stop=True).then_inc(b_ps, 1)
            pe.wait_ge(b_col, 2)
            nc.tensor.transpose(ps[0:1, AUX_BANK, 0:B], bmax[:, :], ident_s[0:B, 0:B]).then_inc(b_ps, 1)
            pe.wait_ge(flag_ready, 1)
            unbounded = pe.value_load(flag[0:1, 0:1], min_val=0, max_val=1)
            with pe.If(unbounded):
                pe.wait_ge(loaded["wo"], 16)
                with pe.Fori(0, B // 2) as i:
                    for par in range(2):
                        b = i * 2 + par
                        again = i * 2 + (B + par)
                        pe.wait_ge(g_ctx_loaded, b * 16 + 16)
                        for c, (m0, mn) in enumerate(KCH):
                            last = nc.tensor.matmul(ps[:, c, 0:mn], wk_s[:, :], g_ctx[:, m0:m0 + mn], start=True, stop=True)
                        last.then_inc(g_k_ps, 1)
                        for t in range(KT):
                            mn = min(P, M - t * P)
                            last = nc.tensor.matmul(ps[0:mn, 4 + t // 4, (t % 4) * D:(t % 4 + 1) * D],
                                                    g_ctx[:, t * P:t * P + mn], wv_s[:, :], start=True, stop=True)
                        last.then_inc(g_v_ps, 1)
                        xT(again, job(b, "T", "again"))
                        queries(job(b, "Q", "again"))
                        pe.wait_ge(g_k_done, b * 2 + 2)
                        pe.wait_ge(g_v_done, b * 2 + 2)
                        pe.wait_ge(g_qbd_done, b + 1)
                        for h in range(H):
                            if h:
                                pe.wait_ge(g_exp, b * H + h)
                            for c in range(4):
                                last = nc.tensor.matmul(ps[0:N, c, 0:M // 4], g_qbd[:, h, :],
                                                        g_kT[:, c * (M // 4):(c + 1) * (M // 4)], start=True, stop=True)
                            last.then_inc(g_s_ps, 1)
                            pe.wait_ge(g_exp, b * H + h + 1)
                            for t in range(KT):
                                mn = min(P, M - t * P)
                                last = nc.tensor.transpose(ps[0:mn, 4 + t // 4, (t % 4) * D:(t % 4) * D + N],
                                                           g_p[:, t * P:t * P + mn], ident_s[0:N, 0:N])
                            last.then_inc(g_pt_ps, 1)
                            pe.wait_ge(g_pt_done, (b * H + h + 1) * 3)
                            for t in range(KT):
                                mn = min(P, M - t * P)
                                last = nc.tensor.matmul(ps[0:N, AUX_BANK, h * HD:(h + 1) * HD], g_pT[0:mn, t, :],
                                                        g_v[0:mn, t, h * HD:(h + 1) * HD], start=(t == 0),
                                                        stop=(t == KT - 1))
                            last.then_inc(g_o_ps, 1)
                        pe.wait_ge(g_o_done, b + 1)
                        nc.tensor.transpose(ps[:, AUX_BANK, 128:128 + N], g_o, ident_s[0:N, 0:N]).then_inc(g_ot_ps, 1)
                        pe.wait_ge(g_chain, b * (H + 2) + H + 2)
                        n = job(b, "O", "again")
                        pe.wait_ge(aux_free, n)
                        nc.tensor.matmul(ps[0:N, AUX_BANK, 0:D], g_oT, wo_s[:, :], start=True, stop=True).then_inc(aux_ps, 1)
                        rowsT(again, par, job(b, "R0", "again"))
                        logits(job(b, "R1", "again"))
                        ranks(again, job(b, "R2", "again"))

            def turn(k, j):
                pe.wait_ge(f_norm, k + 1)
                nc.tensor.transpose(ps[:, j % 2, 0:P], f_n[j % 2], ident_s[:, :]).then_inc(f_T_ps, 1)

            def hidden(k, j, half):
                pe.wait_ge(f_T, k + 1)
                pe.wait_ge(w_loaded[j], half * 16 + 16)
                for c in range(FC):
                    ins = nc.tensor.matmul(ps[:, HIDDEN[j % 2] + c // 2, (c % 2) * P:(c % 2 + 1) * P],
                                           w_t[j][:, c * P:(c + 1) * P], f_x[j % 2], start=True, stop=True)
                    if c % 2:
                        ins.then_inc(f_h_ps, 1)

            def result(k, j):
                o = ps[:, 4 + j % 2, 0:D]
                w2 = w_t[j][:, F:F + FC * D]
                if not isinstance(k, int) or k >= 2:
                    pe.wait_ge(f_half, k - 1)
                nc.tensor.matmul(o, ones_s[:, :], w_t[j][0:1, PACK - D:PACK], start=True, stop=False)
                for c in range(FC):
                    pe.wait_ge(f_hid, k * FC + c + 1)
                    last = nc.tensor.matmul(o, f_h[j % 2][:, c, :], w2[:, c * D:(c + 1) * D], start=False, stop=(c == FC - 1))
                last.then_inc(f_y_ps, 1)

            turn(0, 0)
            hidden(0, 0, 0)
            turn(1, 1)

            def step(k, j, half):
                hidden(k + 1, (j + 1) % TB, half + (j + 1) // TB)
                turn(k + 2, (j + 2) % TB)
                result(k, j)

            for j in range(TB):
                step(j, j, 0)
            with pe.Fori(1, TILES // TB - 1) as i:
                for j in range(TB):
                    step(i * TB + j, j, i)
            for k in range(TILES - TB, TILES - 2):
                step(k, k % TB, TILES // TB - 1)
            hidden(TILES - 1, TB - 1, TILES // TB - 1)
            result(TILES - 2, TB - 2)
            result(TILES - 1, TB - 1)


def kernel(x, ctx_1024, L0_xattn_wq, L0_xattn_wk, L0_xattn_wv, L0_xattn_wo, L0_xattn_bo, L0_ffn_centroids,
           L0_ffn_ln_g, L0_ffn_ln_b, L0_ffn_W1, L0_ffn_b1, L0_ffn_W2, L0_ffn_b2):
    import numpy as np
    import concourse.bacc as bacc
    from concourse.bass_utils import run_bass_kernel_spmd

    def lay(a):
        return np.ascontiguousarray(np.asarray(a))

    woT = lay(np.asarray(L0_xattn_wo).T)
    wox = np.zeros((4, 32, 2, 2, D), np.float32)
    for half in range(2):
        for side in range(2):
            wox[:, side * HD:(side + 1) * HD, half, side, :] = woT.reshape(2, 4, 2, HD, D)[half, :, side]
    pack = np.zeros((E, P, PACK), np.float32)
    pack[:, :, 0:F] = np.asarray(L0_ffn_W1)
    pack[:, :, F:F + FC * D] = np.asarray(L0_ffn_W2).reshape(E, FC, P, D).transpose(0, 2, 1, 3).reshape(E, P, FC * D)
    g0 = F + FC * D
    pack[:, :, g0] = np.asarray(L0_ffn_ln_g)
    pack[:, :, g0 + 1] = np.asarray(L0_ffn_ln_b)
    pack[:, :, g0 + 2:g0 + 2 + FC] = np.asarray(L0_ffn_b1).reshape(E, FC, P).transpose(0, 2, 1)
    pack[:, 0, PACK - D:] = np.asarray(L0_ffn_b2)
    pad_row = np.zeros((P, ROW), np.float32)
    pad_row[:, 2 * D:].view(np.int32)[:] = 1 << 20
    before = np.arange(N)
    arrays = {
        "x": lay(x),
        "ctxT": lay(np.asarray(ctx_1024).transpose(0, 2, 1)),
        "wqT": lay(np.asarray(L0_xattn_wq).T), "wkT": lay(np.asarray(L0_xattn_wk).T),
        "wvT": lay(np.asarray(L0_xattn_wv).T), "woT": woT, "wox": wox.reshape(P, 4, D),
        "bo": lay(np.broadcast_to(np.asarray(L0_xattn_bo), (N, D))),
        "centT": lay(np.asarray(L0_ffn_centroids).T),
        "pack": pack,
        "ident": np.eye(P, dtype=np.float32),
        "rank": np.broadcast_to(np.arange(E, 0, -1, dtype=np.float32), (N, E)).copy(),
        "headmask": np.kron(np.eye(H, dtype=np.float32), np.ones((HD, 1), np.float32)),
        "lower": np.stack([(before[:, None] < before[None, :]), np.ones((N, N), bool)], 1).astype(np.float32),
        "ids": (np.arange(B, dtype=np.int32)[None, :] * N + np.arange(N, dtype=np.int32)[:, None]),
        "first_row": np.broadcast_to(np.arange(E, dtype=np.float32) * REGION, (N, E)).copy(),
        "prefix": (np.arange(E + 1)[:, None] > np.arange(E)[None, :]).astype(np.float32)[None],
        "tile_row": np.arange(TILES, dtype=np.float32)[None],
        "pad_row": pad_row,
    }
    nc = bacc.Bacc("TRN2", target_bir_lowering=False, num_devices=1)
    ins = [nc.dram_tensor(f"in_{n}", a.shape, mybir.dt.from_np(a.dtype), kind="ExternalInput").ap()
           for n, a in arrays.items()]
    out = nc.dram_tensor("out_x", (B, N, D), F32, kind="ExternalOutput").ap()
    build(nc, *ins, out)
    r = run_bass_kernel_spmd(nc, [{f"in_{n}": a for n, a in arrays.items()}], core_ids=[0])
    return r.results[0]["out_x"]
```

```python
from contextlib import ExitStack

import concourse.bass as bass
from concourse import mybir

F32 = mybir.dt.float32
BF16 = mybir.dt.bfloat16
I32 = mybir.dt.int32
ALU = mybir.AluOpType
ACT = mybir.ActivationFunctionType
AX = mybir.AxisListType

B, N, D = 32, 100, 128
M = 1444
H, HD = 16, 8
P = 128
E, F = 8, 512
FC = F // P
KT = -(-M // P)
MPAD = KT * P
LAST = M - (KT - 1) * P
SCALE = float(HD) ** -0.5
EPS = 1e-5
KCH = [(0, 482), (482, 482), (964, 480)]
KC = len(KCH)
VCH = 4
HP = H // 2
VW = 2 * HD + 1
UNITS = 16
UB = 3
TERMS = [(0, 0), (0, 1), (0, 2), (1, 0), (1, 1), (2, 0)]
ROWS = len(TERMS) * 2 * HD
RUNS = [(0, 3), (3, 2), (5, 1)]
AHEAD = 2
PSLOTS = 4
THRESHOLD = 60.0
O_BANK, AUX_BANK = 6, 7

JOBS = ["V0", "V1", "V2", "K0", "K1", "K2", "O", "T", "Q", "R0", "R1", "R2"]
PREPARE = ["K0", "K1", "K2", "T", "Q"]
SLOT = {"V0": 0, "V1": 1, "V2": 2, "B0": 3, "B1": 5, "K0": 3, "K1": 5, "K2": 7, "O": 8.5, "T": 10, "Q": 11,
        "R0": 12.5, "R1": 13.5, "R2": 14.5}
FIRST_SLOT = {"K0a": 0, "K1a": 2, "K2a": 3.5, "Ta": 5, "Qa": 6, "V0": 7, "V1": 8, "V2": 9, "K0": 10, "K1": 12, "K2": 13.5,
              "T": 14.5, "Q": 15}
EARLY_BANK = {"K0": 0, "K1": 1, "K2": 2, "V0": 3, "V1": 4, "V2": 5}
KINDS = {
    "before": [*PREPARE, "V0", "V1", "V2"],
    "first": [*(n + "a" for n in PREPARE), *(n for n in JOBS if n[0] in "VKTQ")],
    "middle": JOBS,
    "late": ["V0", "V1", "V2", "B0", "B1", "O", "R0", "R1", "R2"],
    "last": [n for n in JOBS if n[0] in "OR"],
    "after": [n for n in JOBS if n[0] in "OR"],
    "again": ["T", "Q", "O", "R0", "R1", "R2"],
}
FIRST_JOB, BASE = {}, 0
for _kind, _batches in (("before", 1), ("first", 1), ("middle", B - 3), ("late", 1), ("last", 1),
                        ("after", 1), ("again", B)):
    FIRST_JOB[_kind], BASE = BASE, BASE + _batches * len(KINDS[_kind])


def job(b, name, kind):
    at = FIRST_JOB[kind] + KINDS[kind].index(name)
    if kind == "middle":
        return (b - 1) * len(JOBS) + at
    if kind == "again":
        return b * len(KINDS[kind]) + at
    return at


ROW = 2 * D + 1
PADS = -(-(2 * N + P) // P)
REGION = B * N + PADS * P
TILES = (B * N) // P + E - 1
OB = 4
TB = 8
HIDDEN = (2, 6)
PACK = 2 + FC + F
ARENA = 30052


def build(nc, x, ctxT, wqT, wkT, wvT, woT, wox, sides, bo, centT, pack, w2, b2, ident, rank, headmask, lower, ids, first_row,
          prefix, tile_row, pad_row, out):
    with ExitStack() as stack:
        def sb(name, shape, dt=F32):
            return stack.enter_context(nc.sbuf_tensor(name, shape, dt))

        def sems(names):
            return [stack.enter_context(nc.semaphore(n)) for n in names.split()]

        ps = stack.enter_context(nc.psum_tensor("ps", [P, 8, 512], F32))

        wq_s, wk_s, wv_s, wo_s = (sb(n, [D, D]) for n in ("wq_s", "wk_s", "wv_s", "wo_s"))
        wox_s = sb("wox_s", [P, 2, D])
        sides_s = sb("sides_s", [P, 2])
        bo_s = sb("bo_s", [N, D])
        cent_s = sb("cent_s", [D, E])
        ident_s = sb("ident_s", [P, P])
        rank_s = sb("rank_s", [N, E])
        headmask_s = sb("headmask_s", [D, H])
        lower_s = sb("lower_s", [N, 2, N])
        ids_s = sb("ids_s", [N, B], I32)
        first_s = sb("first_s", [N, E])
        prefix_s = sb("prefix_s", [1, E, E])
        tile_row_s = sb("tile_row_s", [1, TILES])
        pad_s = sb("pad_s", [P, ROW])
        w2_s, b2_s = sb("w2_s", [P, E, FC * D]), sb("b2_s", [P, E, D])
        half_s, eps_s = sb("half_s", [P, 1]), sb("eps_s", [P, 1])
        credit = sb("credit", [1, 12])
        x_s = sb("x_s", [N, B, D])
        x_stats, x_mv, x_var, x_rstd = (sb(n, [N, w]) for n, w in (("x_stats", 6), ("x_mv", 2), ("x_var", 1), ("x_rstd", 1)))
        xn, xnT = sb("xn", [N, D]), sb("xnT", [D, N])
        qparts, qrest = sb("qparts", [D, 3, N], BF16), sb("qrest", [D, N])
        rows = [sb(f"row{k}", [N, ROW]) for k in range(2)]
        r_stats, r_mv, r_var, r_rstd = (sb(n, [N, w]) for n, w in (("r_stats", 6), ("r_mv", 2), ("r_var", 1), ("r_rstd", 1)))
        y_stats, y_mv, y_var, y_rstd = (sb(n, [N, w]) for n, w in (("y_stats", 6), ("y_mv", 2), ("y_var", 1), ("y_rstd", 1)))
        x1_s, y_s, yT = sb("x1_s", [N, D]), sb("y_s", [N, D]), sb("yT", [D, N])
        lmax, lfirst, slot_f = (sb(n, [N, 1]) for n in ("lmax", "lfirst", "slot_f"))
        leq, lrank, onehot, place, picked = (sb(n, [N, E]) for n in ("leq", "lrank", "onehot", "place", "picked"))
        slot_i = [sb(f"slot_i{k}", [N, 1], I32) for k in range(2)]
        run = sb("run", [N, E])
        qmax, kmax, bound = sb("qmax", [D, B]), sb("kmax", [D, KC, B]), sb("bound", [D, B])
        kall = sb("kall", [D, B])
        bmax, btop, bok = sb("bmax", [B, 1]), sb("btop", [1, 1]), sb("bok", [1, 1])
        flag = sb("flag", [1, 1], I32)
        t_num, t_skip, t_cum = (sb(n, [1, E]) for n in ("t_num", "t_skip", "t_cum"))
        t_int = sb("t_int", [1, E], I32)
        t_pre, t_ge = sb("t_pre", [1, E, E]), sb("t_ge", [1, TILES, E])
        t_exp, t_row = sb("t_exp", [1, TILES]), sb("t_row", [1, TILES])
        table = sb("table", [1, 2, TILES], I32)
        t_pad = sb("t_pad", [1, E], I32)
        arena = sb("arena", [P, ARENA])

        class Carver:
            def __init__(self):
                self.at = 0

            def __call__(self, shape, dt=F32):
                n = 1
                for k in shape[1:]:
                    n *= k
                words = n if dt == F32 else -(-n // 2)
                assert self.at + words <= ARENA
                ap = arena[0:shape[0], self.at:self.at + words]
                self.at += words
                if dt != F32:
                    ap = ap.bitcast(dt)
                names = "abcde"[:len(shape) - 1]
                if len(names) > 1:
                    ap = ap.rearrange(f"p ({' '.join(names)}) -> p {' '.join(names)}", **dict(zip(names, shape[1:])))
                return ap

        cut = Carver()
        ks = [cut([ROWS, HP, MPAD], BF16) for _ in range(2)]
        qs = [cut([ROWS, HP, 2 * N], BF16) for _ in range(2)]
        kparts = cut([D, 3, M], BF16)
        krest = [cut([D, KCH[0][1]]) for _ in range(KC)]
        ctx_s = [cut([D, M]) for _ in range(2)]
        va = [cut([P, KT, HP, VW]) for _ in range(2)]
        probs = [cut([P, UB, 4 * N]) for _ in range(PSLOTS)]
        o_raw, o_sum = (cut([P, 4 * N]) for _ in range(2))
        o_tmp, o_pick, s_pick, o_norm = (cut([P, 2 * N]) for _ in range(4))
        cut = Carver()
        g_ctx, g_kT, g_v, g_qbd = cut([D, M]), cut([D, M]), cut([P, KT, D]), cut([D, H, N])
        g_p, g_pT = cut([N, M]), cut([P, KT, N])
        smax, nbias, ssum, sinv = (cut([N, H]) for _ in range(4))
        g_o, g_oT, g_qT = cut([N, D]), cut([D, N]), cut([D, N])
        cut = Carver()
        y_t = [cut([P, ROW]) for _ in range(TB)]
        w_t = [cut([P, PACK]) for _ in range(TB)]
        f_x = [cut([D, P]) for _ in range(2)]
        f_h = [cut([P, FC, P]) for _ in range(2)]
        f_o = [cut([P, D]) for _ in range(OB)]

        k_dram = [nc.dram_tensor(f"k_dram{i}", (3, D, M), BF16).ap() for i in range(2)]
        QW = HP * 2 * N
        q_dram = [nc.dram_tensor(f"q_dram{i}", ((3 + HP - 1) * 2 * HD, QW), BF16).ap() for i in range(2)]
        y_dram = nc.dram_tensor("y_dram", (E * REGION + P, ROW), F32).ap()

        consts = [("wk", wk_s[:, :], wkT), ("x0", x_s[:, 0:2, :], x[0:2].rearrange("b n d -> n b d")),
                  ("bo", bo_s[:, :], bo), ("ident", ident_s[:, :], ident), ("wq", wq_s[:, :], wqT), ("wv", wv_s[:, :], wvT),
                  ("pad", pad_s[:, :], pad_row), ("wox", wox_s[:, :, :], wox), ("sides", sides_s[:, :], sides),
                  ("cent", cent_s[:, :], centT), ("rank", rank_s[:, :], rank), ("lower", lower_s[:, :, :], lower),
                  ("ids", ids_s[:, :], ids), ("run", run[:, :], first_row), ("first", first_s[:, :], first_row),
                  ("headmask", headmask_s[:, :], headmask), ("prefix", prefix_s[:, :, :], prefix),
                  ("tile_row", tile_row_s[:, :], tile_row), ("wo", wo_s[:, :], woT),
                  ("x1", x_s[:, 2:B, :], x[2:B].rearrange("b n d -> n b d")), ("w2", w2_s[:, :, :], w2),
                  ("b2", b2_s[:, :, :], b2)]
        loaded = {name: sem for (name, _, _), sem in zip(consts, sems(" ".join(f"load_{c[0]}" for c in consts)))}

        pads_done, zeroed, consts_ready = sems("pads_done zeroed consts_ready")
        ctx_loaded, ks_loaded, qs_loaded, row_stored = (
            sems(f"{n}0 {n}1") for n in ("ctx_loaded", "ks_loaded", "qs_loaded", "row_stored"))
        aux_ps, aux_free, v_part = sems("aux_ps aux_free v_part")
        x_chain, x_var_in, x_std, x_norm, q_chain, q_split, q_cleared = sems(
            "x_chain x_var_in x_std x_norm q_chain q_split q_cleared")
        q_stored = sems("q_stored0 q_stored1 q_stored2")
        k_steps, k_split, k_stored, kmax_done = sems("k_steps k_split k_stored kmax_done")
        sc_ps, exp_done, pv_done = sems("sc_ps exp_done pv_done")
        o_copied, o_steps, o_ready = sems("o_copied o_steps o_ready")
        r_chain, r_var_in, r_std, r_norm, r_hot, r_slot, r_id, p_chain, rp_chain = sems(
            "r_chain r_var_in r_std r_norm r_hot r_slot r_id p_chain rp_chain")
        y_var_in, y_std, yp_chain, z_done, r_row = sems("y_var_in y_std yp_chain z_done r_row")
        b_chain, b_col, flag_ready = sems("b_chain b_col flag_ready")
        g_x, g_ctx_loaded, g_k_ps, g_k_done, g_v_ps, g_v_done, g_qbd_done, g_reset, g_pause = sems(
            "g_x g_ctx_loaded g_k_ps g_k_done g_v_ps g_v_done g_qbd_done g_reset g_pause")
        g_s_ps, g_bias, g_exp, g_pt_ps, g_pt_done, g_o_ps, g_o_done, g_ot_ps, g_ot_done, g_chain = sems(
            "g_s_ps g_bias g_exp g_pt_ps g_pt_done g_o_ps g_o_done g_ot_ps g_ot_done g_chain")
        t_chain, t_ready, pad_ready, pads_stored, rows_done = sems("t_chain t_ready pad_ready pads_stored rows_done")
        y_loaded, w_loaded = (sems(" ".join(f"{n}{k}" for k in range(TB))) for n in ("y_loaded", "w_loaded"))
        out_stored = sems("out_stored0 out_stored1 out_stored2 out_stored3")
        f_T_ps, f_T, f_h_ps, f_hid, f_y_ps, f_half, f_o_done = sems("f_T_ps f_T f_h_ps f_hid f_y_ps f_half f_o_done")

        X_STEPS, R_STEPS, Q_STEPS, O_STEPS = 2, 8, 3, 6
        block = stack.enter_context(nc.Block())

        class Chain:
            def __init__(self, eng, s, i, per):
                self.eng, self.s, self.i, self.per, self.n = eng, s, i, per, 0

            def __call__(self, ins):
                self.n += 1
                assert self.n <= self.per
                ins.then_inc(self.s, 1)
                self.eng.wait_ge(self.s, self.i * self.per + self.n)

        @block.gpsimd
        def _(pool):
            for k in range(2):
                nc.gpsimd.memset(va[k][:, 0:KT - 1, :, VW - 1:VW], 1.0).then_inc(pads_done, 1)
                nc.gpsimd.memset(va[k][:, KT - 1, :, :], 0.0).then_inc(zeroed, 1)
                pool.wait_ge(zeroed, k + 1)
                nc.gpsimd.memset(va[k][0:LAST, KT - 1, :, VW - 1:VW], 1.0).then_inc(pads_done, 1)
                nc.gpsimd.memset(ks[k][:, :, M:MPAD], 0.0).then_inc(pads_done, 1)
            pool.wait_ge(consts_ready, 4)

            def met():
                pool.wait_ge(consts_ready, 4)

            def last_part(kb, j):
                m0, mn = KCH[j]
                pool.wait_ge(k_steps, kb * 2 * KC + 2 * j + 2)
                nc.gpsimd.tensor_tensor(kparts[:, 2, m0:m0 + mn], krest[j][:, 0:mn], kparts[:, 1, m0:m0 + mn],
                                        ALU.subtract).then_inc(k_split, 1)

            def query_norm(kb):
                pool.wait_ge(x_var_in, kb + 1)
                nc.gpsimd.tensor_tensor(x_var[:, :], x_mv[:, 1:2], eps_s[0:N, :], ALU.add).then_inc(p_chain, 1)
                pool.wait_ge(p_chain, kb + 1)
                nc.gpsimd.tensor_tensor(x_rstd[:, :], x_var[:, :], half_s[0:N, :], ALU.pow).then_inc(x_std, 1)

            def row_norm(b):
                pool.wait_ge(r_var_in, b + 1)
                nc.gpsimd.tensor_tensor(r_var[:, :], r_mv[:, 1:2], eps_s[0:N, :], ALU.add).then_inc(rp_chain, 1)
                pool.wait_ge(rp_chain, b + 1)
                nc.gpsimd.tensor_tensor(r_rstd[:, :], r_var[:, :], half_s[0:N, :], ALU.pow).then_inc(r_std, 1)

            def store_rows(b, data, par, before):
                pool.wait_ge(r_norm, b + 1)
                pool.wait_ge(row_stored[par], before * 16 + 16)
                nc.gpsimd.tensor_tensor(rows[par][:, D:2 * D], x1_s[:, :], y_s[:, :], ALU.add).then_inc(z_done, 1)
                pool.wait_ge(y_var_in, b + 1)
                nc.gpsimd.tensor_tensor(y_var[:, :], y_mv[:, 1:2], eps_s[0:N, :], ALU.add).then_inc(yp_chain, 1)
                pool.wait_ge(yp_chain, b + 1)
                nc.gpsimd.tensor_tensor(y_rstd[:, :], y_var[:, :], half_s[0:N, :], ALU.pow).then_inc(y_std, 1)
                nc.gpsimd.tensor_copy(rows[par][:, 2 * D:2 * D + 1].bitcast(I32), ids_s[:, bass.ds(data, 1)])\
                    .then_inc(r_id, 1)
                met()
                for s in (z_done, r_id, r_row, r_slot):
                    pool.wait_ge(s, b + 1)
                nc.gpsimd.indirect_dma_start(y_dram, bass.IndirectOffsetOnAxis(ap=slot_i[par][:, 0:1], axis=0),
                                             rows[par][:, :], None).then_inc(row_stored[par], 16)

            def prepare(kb):
                last_part(kb, 0)
                last_part(kb, 1)
                query_norm(kb)
                last_part(kb, 2)

            def finish_rows(b, par, before):
                row_norm(b)
                store_rows(b, b, par, before)

            prepare(0)
            for name in ("ids", "pad"):
                pool.wait_ge(loaded[name], 16)
            for k in range(2):
                nc.gpsimd.dma_start(y_dram[E * REGION + k * P // 2:E * REGION + (k + 1) * P // 2, :],
                                    pad_s[k * P // 2:(k + 1) * P // 2, :]).then_inc(row_stored[k], 16)
            prepare(1)
            prepare(2)
            with pool.Fori(0, B // 2 - 2) as i:
                prepare(i * 2 + 3)
                finish_rows(i * 2, 0, i)
                prepare(i * 2 + 4)
                finish_rows(i * 2 + 1, 1, i)
            prepare(B - 1)
            for b in range(B - 4, B):
                if b == B - 2:
                    pool.wait_ge(pads_stored, E * 16)
                finish_rows(b, b % 2, b // 2)

            pool.wait_ge(flag_ready, 1)
            unbounded = pool.value_load(flag[0:1, 0:1], min_val=0, max_val=1)
            with pool.If(unbounded):
                with pool.Fori(0, B // 2) as i:
                    for par in range(2):
                        query_norm(i * 2 + (B + par))
                        row_norm(i * 2 + (B + par))
                        store_rows(i * 2 + (B + par), i * 2 + par, par, i + B // 2)

            def tile_out(k, j):
                pool.wait_ge(f_half, k + 1)
                nc.gpsimd.tensor_tensor(f_o[j % OB], f_o[j % OB], y_t[j][:, D:2 * D], ALU.add).then_inc(f_o_done, 1)
                met()
                pool.wait_ge(f_o_done, k + 1)
                nc.gpsimd.indirect_dma_start(out.rearrange("b n d -> (b n) d"),
                                             bass.IndirectOffsetOnAxis(ap=y_t[j][:, 2 * D:2 * D + 1].bitcast(I32), axis=0),
                                             f_o[j % OB], None, bounds_check=B * N - 1, oob_is_err=False)\
                    .then_inc(out_stored[j % OB], 16)

            with pool.Fori(0, TILES // TB) as i:
                for j in range(TB):
                    tile_out(i * TB + j, j)
            for k in range(OB):
                pool.wait_ge(out_stored[k], TILES // OB * 16)

        @block.sync
        def _(sp):
            def load(first, last):
                for name, dst, src in consts[first:last]:
                    sp.dma_start(dst, src).then_inc(loaded[name], 16)

            load(0, 1)
            sp.dma_start(ctx_s[0], ctxT[0]).then_inc(ctx_loaded[0], 16)
            load(1, 6)
            sp.dma_start(ctx_s[1], ctxT[1]).then_inc(ctx_loaded[1], 16)
            sp.wait_ge(pads_done, 6)
            sp.wait_ge(consts_ready, 4)
            more = q_dram[0].shape[0] - ROWS
            for p in range(2):
                sp.dma_start(q_dram[p][0:ROWS, :], qs[p].rearrange("r p n -> r (p n)")).then_inc(q_cleared, 16)
                sp.dma_start(q_dram[p][ROWS:, :], qs[p][0:more].rearrange("r p n -> r (p n)")).then_inc(q_cleared, 16)
            load(6, len(consts) - 3)
            sp.wait_ge(q_cleared, 4 * 16)

            def context(kb, par, jobs_done):
                sp.wait_ge(aux_ps, jobs_done)
                sp.dma_start(ctx_s[par], ctxT[bass.ds(kb, 1)].squeeze(0)).then_inc(ctx_loaded[par], 16)

            def operands(kb, par, recycled):
                sp.wait_ge(k_split, (kb + 1) * KC)
                sp.dma_start(k_dram[par].rearrange("t d m -> d t m"), kparts).then_inc(k_stored, 16)
                sp.wait_ge(q_split, kb + 1)
                for t in range(3):
                    sp.dma_start(bass.AP(q_dram[par].tensor, t * 2 * HD * QW, [[HD * QW + N, H], [QW, HD], [1, N]]),
                                 qparts[:, t, :]).then_inc(q_stored[t], 16)
                sp.wait_ge(k_stored, (kb + 1) * 16)
                for t in range(3):
                    sp.wait_ge(q_stored[t], (kb + 1) * 16)
                if recycled:
                    sp.wait_ge(sc_ps, (kb + 1) * UNITS)
                for t, (part, _) in enumerate(TERMS):
                    src = k_dram[par][part].rearrange("(p r) m -> r p m", p=HP)
                    sp.dma_start(ks[par][2 * t * HD:2 * (t + 1) * HD, :, 0:M], src).then_inc(ks_loaded[par], 16)
                for t0, n in RUNS:
                    sp.dma_start(qs[par][t0 * 2 * HD:(t0 + n) * 2 * HD],
                                 bass.AP(q_dram[par].tensor, 0, [[QW, n * 2 * HD], [2 * HD * QW + 2 * N, HP], [1, 2 * N]]))\
                        .then_inc(qs_loaded[par], 16)

            operands(0, 0, False)
            context(2, 0, job(0, "V2", "before") + 1)
            load(len(consts) - 3, len(consts) - 2)
            operands(1, 1, False)
            context(3, 1, job(0, "V2", "first") + 1)
            operands(2, 0, True)
            load(len(consts) - 2, len(consts))
            with sp.Fori(0, B // 2 - 2) as i:
                for p in range(2):
                    b = i * 2 + (p + 1)
                    context(b + 3, p, job(b, "V2", "middle") + 1)
                    operands(b + 2, 1 - p, True)
            operands(B - 1, 1, True)

            def store_pads(count):
                sp.wait_ge(pad_ready, count)
                for e in range(E):
                    row = sp.value_load(t_pad[0:1, e:e + 1], min_val=e * REGION, max_val=(e + 1) * REGION - PADS * P)
                    sp.dma_start(y_dram[bass.ds(row, PADS * P), :].rearrange("(a p) w -> p a w", p=P),
                                 pad_s[:, :].unsqueeze(1).to_broadcast([P, PADS, ROW])).then_inc(pads_stored, 16)

            store_pads(1)
            sp.wait_ge(flag_ready, 1)
            unbounded = sp.value_load(flag[0:1, 0:1], min_val=0, max_val=1)
            with sp.If(unbounded):
                sp.wait_ge(r_norm, B)
                sp.dma_start(x_s[:, :, :], x.rearrange("b n d -> n b d")).then_inc(g_x, 16)
                with sp.Fori(0, B) as b:
                    sp.wait_ge(g_v_ps, b + 1)
                    sp.dma_start(g_ctx, ctxT[b]).then_inc(g_ctx_loaded, 16)
                store_pads(2)
                sp.wait_ge(pads_stored, 2 * E * 16)

            def tile(k, j, reused):
                if reused is not None:
                    sp.wait_ge(out_stored[j % OB], reused)
                row = sp.value_load(table[0:1, 1, bass.ds(k, 1)], min_val=0, max_val=E * REGION)
                sp.dma_start(y_t[j], y_dram[bass.ds(row, P), :]).then_inc(y_loaded[j], 16)
                if reused is None or j % 2 == 0:
                    expert = sp.value_load(table[0:1, 0, bass.ds(k, 1)], min_val=0, max_val=E - 1)
                    sp.dma_start(w_t[j], pack[bass.ds(expert, 1)].squeeze(0)).then_inc(w_loaded[j], 16)

            sp.wait_ge(t_ready, 2)
            sp.wait_ge(rows_done, 1)
            for j in range(TB):
                tile(j, j, None)
            with sp.Fori(0, TILES // TB - 1) as i:
                for j in range(TB):
                    tile(i * TB + (TB + j), j, (i * (TB // OB) + j // OB) * 16 + 16)

        @block.scalar
        def _(act):
            def exponentials(b):
                for u in range(UNITS):
                    act.wait_ge(sc_ps, b * UNITS + (u + 1 + 2 * UNITS))
                    act.wait_ge(pv_done, b * UNITS + u + 1)
                    r = UB * (u % 2)
                    nc.scalar.activation(probs[u % PSLOTS], ps[:, r:r + UB, 0:4 * N], ACT.Exp, scale=SCALE)\
                        .then_inc(exp_done, 1)

            exponentials(0)
            with act.Fori(1, B) as b:
                exponentials(b)

            act.wait_ge(flag_ready, 1)
            unbounded = act.value_load(flag[0:1, 0:1], min_val=0, max_val=1)
            with act.If(unbounded):
                with act.Fori(0, B) as b:
                    for h in range(H):
                        act.wait_ge(g_bias, b * H + h + 1)
                        if h:
                            act.wait_ge(g_pt_ps, b * H + h)
                        nc.scalar.activation(g_p.rearrange("n (c m) -> n c m", c=4),
                                             ps[0:N, 0:4, 0:M // 4], ACT.Exp, bias=nbias[:, h:h + 1],
                                             scale=SCALE, accum_out=ssum[:, h:h + 1]).then_inc(g_exp, 1)

            def hidden(k, j, half):
                act.wait_ge(w_loaded[j], half * 16 + 16)
                for c in range(FC):
                    if c % 2 == 0:
                        act.wait_ge(f_h_ps, k * 2 + (c // 2 + 1))
                    if c == 0:
                        act.wait_ge(f_y_ps, k + 1)
                    nc.scalar.activation(f_h[j % 2][:, c, :],
                                         ps[:, HIDDEN[j % 2] + c // 2, (c % 2) * P:(c % 2 + 1) * P], ACT.Relu, bias=w_t[j][:, 2 + c:3 + c]).then_inc(f_hid, 1)

            def weights(k, j, n):
                act.wait_ge(f_hid, n)
                expert = act.value_load(table[0:1, 0, bass.ds(k + TB, 1)], min_val=0, max_val=E - 1)
                act.dma_start(w_t[j], pack[bass.ds(expert, 1)].squeeze(0)).then_inc(w_loaded[j], 16)

            with act.Fori(0, TILES // TB - 1) as i:
                for j in range(TB):
                    hidden(i * TB + j, j, i)
                    if j % 2 == 0 and j:
                        weights(i * TB + (j - 1), j - 1, (i * TB + j) * FC)
                weights(i * TB + (TB - 1), TB - 1, (i * TB + TB) * FC)
            for j in range(TB):
                hidden(TILES - TB + j, j, TILES // TB - 1)

        @block.vector
        def _(dve):
            nc.vector.memset(half_s[:, :], -0.5).then_inc(consts_ready, 1)
            nc.vector.memset(eps_s[:, :], EPS).then_inc(consts_ready, 1)
            nc.vector.memset(qs[0], 0.0).then_inc(consts_ready, 1)
            nc.vector.memset(qs[1], 0.0).then_inc(consts_ready, 1)
            nc.vector.memset(ps[:, O_BANK, :], 0.0).then_inc(o_copied, 1)
            for k, (s, n) in enumerate([(pv_done, PSLOTS), (sc_ps, 2 * UNITS), (o_ready, 1), (g_v_ps, 1), (f_y_ps, 2),
                                        (g_pause, 1)]):
                nc.vector.memset(credit[0:1, k:k + 1], 0.0).then_inc(s, n)
            for name in ("x0", "bo"):
                dve.wait_ge(loaded[name], 16)

            def query_stats(kb, data):
                link = Chain(dve, x_chain, kb, X_STEPS)
                link(nc.vector.bn_stats(x_stats[:, :], x_s[:, bass.ds(data, 1), :].squeeze(1)))
                return link

            def query_variance():
                nc.vector.bn_aggr(x_mv[:, :], x_stats[:, :]).then_inc(x_var_in, 1)

            def query_norm(kb, data):
                xb = x_s[:, bass.ds(data, 1), :].squeeze(1)
                dve.wait_ge(x_std, kb + 1)
                nc.vector.tensor_scalar(xn[:, :], xb, x_mv[:, 0:1], x_rstd[:, :], ALU.subtract, ALU.mult)\
                    .then_inc(x_norm, 1)

            def add_bias(kb, data, link):
                xb = x_s[:, bass.ds(data, 1), :].squeeze(1)
                dve.wait_ge(x_norm, kb + 1)
                link(nc.vector.tensor_tensor(xb, xb, bo_s[:, :], ALU.add))

            def take_xT(n):
                dve.wait_ge(aux_ps, n + 1)
                nc.vector.tensor_copy(xnT[:, :], ps[:, AUX_BANK, 0:N]).then_inc(aux_free, 1)

            def split_queries(kb, n, first=False):
                link = Chain(dve, q_chain, kb, Q_STEPS)
                qp = ps[:, AUX_BANK, 0:N]
                dve.wait_ge(aux_ps, n + 1)
                if not first:
                    for t in range(3):
                        dve.wait_ge(q_stored[t], kb * 16)
                link(nc.vector.tensor_reduce(qmax[:, bass.ds(kb, 1)], qp, AX.X, ALU.max, apply_absolute_value=True))
                link(nc.vector.tensor_copy(qparts[:, 0, :], qp))
                nc.vector.tensor_tensor(qrest[:, :], qp, qparts[:, 0, :], ALU.subtract).then_inc(aux_free, 1)
                dve.wait_ge(aux_free, n + 1)
                link(nc.vector.tensor_copy(qparts[:, 1, :], qrest[:, :]))
                nc.vector.tensor_tensor(qparts[:, 2, :], qrest[:, :], qparts[:, 1, :], ALU.subtract).then_inc(q_split, 1)

            def split_keys(kb, j, n, first, bank=AUX_BANK):
                m0, mn = KCH[j]
                kp = ps[:, bank, 0:mn]
                dve.wait_ge(aux_ps, n + 1)
                if not first:
                    if j == 0:
                        dve.wait_ge(k_stored, kb * 16)
                        dve.wait_ge(kmax_done, kb * KC)
                nc.vector.tensor_copy(kparts[:, 0, m0:m0 + mn], kp).then_inc(k_steps, 1)
                dve.wait_ge(k_steps, kb * 2 * KC + 2 * j + 1)
                nc.vector.tensor_tensor(krest[j][:, 0:mn], kp, kparts[:, 0, m0:m0 + mn], ALU.subtract)\
                    .then_inc(aux_free, 1)
                dve.wait_ge(aux_free, n + 1)
                nc.vector.tensor_copy(kparts[:, 1, m0:m0 + mn], krest[j][:, 0:mn]).then_inc(k_steps, 1)
                nc.vector.tensor_reduce(kmax[:, j, bass.ds(kb, 1)], kparts[:, 0, m0:m0 + mn], AX.X, ALU.max,
                                        apply_absolute_value=True).then_inc(kmax_done, 1)

            def take_values(kb, par, j, n, bank=AUX_BANK):
                t0 = j * VCH
                whole = VCH if j < KT // VCH - 1 else VCH - 1
                dve.wait_ge(aux_ps, n + 1)
                ins = nc.vector.tensor_copy(
                    va[par][:, t0:t0 + whole, :, 0:VW - 1],
                    ps[:, bank, 0:whole * D].rearrange("m (t p d) -> m t p d", t=whole, p=HP))
                if whole == VCH:
                    ins.then_inc(aux_free, 1)
                else:
                    ins.then_inc(v_part, 1)
                    nc.vector.tensor_copy(va[par][0:LAST, KT - 1, :, 0:VW - 1],
                                          ps[0:LAST, bank, whole * D:VCH * D].rearrange("m (p d) -> m p d", p=HP))\
                        .then_inc(aux_free, 1)

            def copy_out(b):
                dve.wait_ge(pv_done, (b + 1) * UNITS + PSLOTS)
                dve.wait_ge(o_ready, b + 1)
                nc.vector.tensor_copy(o_raw, ps[:, O_BANK, 0:4 * N]).then_inc(o_copied, 1)

            def spread_sums(b):
                link = Chain(dve, o_steps, b, O_STEPS)
                link(nc.vector.stream_shuffle(o_sum, o_raw, [2 * HD] * 32))
                return link

            def pick(link, dst, src):
                both = src.rearrange("p (h s n) -> p h s n", h=2, s=2)
                tmp, d = (a.rearrange("p (h n) -> p h n", h=2) for a in (o_tmp, dst))
                link(nc.vector.tensor_scalar(tmp, both[:, :, 0, :], sides_s[:, 0:1], None, ALU.mult))
                link(nc.vector.scalar_tensor_tensor(out=d, in0=both[:, :, 1, :], scalar=sides_s[:, 1:2], in1=tmp,
                                                    op0=ALU.mult, op1=ALU.add))

            def invert(link):
                link(nc.vector.reciprocal(s_pick, s_pick))

            def divide(jobs_done):
                if jobs_done is not None:
                    dve.wait_ge(aux_ps, jobs_done)
                nc.vector.tensor_tensor(o_norm, o_pick, s_pick, ALU.mult).then_inc(o_ready, 1)

            def residual(b, data, n):
                link = Chain(dve, r_chain, b, R_STEPS)
                dve.wait_ge(aux_ps, n + 1)
                nc.vector.tensor_tensor(x1_s[:, :], x_s[:, bass.ds(data, 1), :].squeeze(1), ps[0:N, AUX_BANK, 0:D], ALU.add)\
                    .then_inc(aux_free, 1)
                dve.wait_ge(aux_free, n + 1)
                link(nc.vector.bn_stats(r_stats[:, :], x1_s[:, :]))
                return link

            def row_variance():
                nc.vector.bn_aggr(r_mv[:, :], r_stats[:, :]).then_inc(r_var_in, 1)

            def row_norm(b, link):
                dve.wait_ge(r_std, b + 1)
                nc.vector.tensor_scalar(y_s[:, :], x1_s[:, :], r_mv[:, 0:1], r_rstd[:, :], ALU.subtract, ALU.mult)\
                    .then_inc(r_norm, 1)
                dve.wait_ge(r_norm, b + 1)
                link(nc.vector.bn_stats(y_stats[:, :], y_s[:, :]))

            def y_variance():
                nc.vector.bn_aggr(y_mv[:, :], y_stats[:, :]).then_inc(y_var_in, 1)

            def y_norm(b, par):
                dve.wait_ge(y_std, b + 1)
                nc.vector.tensor_scalar(rows[par][:, 0:D], y_s[:, :], y_mv[:, 0:1], y_rstd[:, :],
                                        ALU.subtract, ALU.mult).then_inc(r_row, 1)

            def take_yT(n):
                dve.wait_ge(aux_ps, n + 1)
                nc.vector.tensor_copy(yT[:, :], ps[:, AUX_BANK, 0:N]).then_inc(aux_free, 1)

            def choose(b, link, n):
                lg = ps[0:N, AUX_BANK, 0:E]
                dve.wait_ge(aux_ps, n + 1)
                link(nc.vector.tensor_reduce(lmax[:, :], lg, AX.X, ALU.max))
                nc.vector.tensor_scalar(leq[:, :], lg, lmax[:, :], None, ALU.is_equal).then_inc(aux_free, 1)
                dve.wait_ge(aux_free, n + 1)
                link(nc.vector.tensor_tensor(lrank[:, :], leq[:, :], rank_s[:, :], ALU.mult))
                link(nc.vector.tensor_reduce(lfirst[:, :], lrank[:, :], AX.X, ALU.max))
                nc.vector.tensor_scalar(onehot[:, :], rank_s[:, :], lfirst[:, :], None, ALU.is_equal).then_inc(r_hot, 1)

            def place_rows(b, par, link, n):
                dve.wait_ge(aux_ps, n + 1)
                link(nc.vector.tensor_tensor(place[:, :], ps[0:N, AUX_BANK, 0:E], run[:, :], ALU.add))
                link(nc.vector.tensor_tensor(picked[:, :], place[:, :], onehot[:, :], ALU.mult))
                link(nc.vector.tensor_reduce(slot_f[:, :], picked[:, :], AX.X, ALU.add))
                nc.vector.tensor_copy(slot_i[par][:, :], slot_f[:, :]).then_inc(r_slot, 1)
                nc.vector.tensor_tensor(run[:, :], run[:, :], ps[0:N, AUX_BANK, E:2 * E], ALU.add).then_inc(aux_free, 1)
                dve.wait_ge(aux_free, n + 1)

            def bound_scores():
                link = Chain(dve, b_chain, 0, 4)
                link(nc.vector.tensor_tensor(kall[:, :], kmax[:, 0, :], kmax[:, 1, :], ALU.max))
                link(nc.vector.tensor_tensor(kall[:, :], kall[:, :], kmax[:, 2, :], ALU.max))
                nc.vector.tensor_tensor(bound[:, :], qmax[:, :], kall[:, :], ALU.mult).then_inc(b_col, 1)
                n = job(B - 2, "B0", "late")
                dve.wait_ge(aux_ps, n + 1)
                nc.vector.tensor_reduce(bmax[:, :], ps[0:B, AUX_BANK, 0:H], AX.X, ALU.max).then_inc(aux_free, 1)
                dve.wait_ge(aux_ps, n + 2)
                nc.vector.tensor_reduce(btop[:, :], ps[0:1, AUX_BANK, 0:B], AX.X, ALU.max).then_inc(aux_free, 1)
                dve.wait_ge(aux_free, n + 2)
                link(nc.vector.tensor_scalar(bok[:, :], btop[:, :], SCALE, THRESHOLD, ALU.mult, ALU.is_le))
                nc.vector.tensor_scalar(flag[:, :], bok[:, :], -1.0, 1.0, ALU.mult, ALU.add).then_inc(flag_ready, 1)

            def batch(b, half, par, kind):
                names = KINDS[kind]
                values, keys, previous = "V0" in names, "K0" in names, "O" in names
                other = 1 - par
                if previous:
                    copy_out(b - 1)
                    dve.wait_ge(o_copied, b + 1)
                if values:
                    take_values(b + 1, other, 0, job(b, "V0", kind))
                if previous:
                    olink = spread_sums(b - 1)
                if values:
                    take_values(b + 1, other, 1, job(b, "V1", kind))
                if previous:
                    pick(olink, s_pick, o_sum)
                    pick(olink, o_pick, o_raw)
                if values:
                    take_values(b + 1, other, 2, job(b, "V2", kind))
                if previous:
                    invert(olink)
                if keys:
                    split_keys(b + 2, 0, job(b, "K0", kind), False)
                if previous:
                    divide(None if values else job(b, "O", kind))
                if keys:
                    xlink = query_stats(b + 2, b + 2)
                    split_keys(b + 2, 1, job(b, "K1", kind), False)
                    query_variance()
                    split_keys(b + 2, 2, job(b, "K2", kind), False)
                    query_norm(b + 2, b + 2)
                    add_bias(b + 2, b + 2, xlink)
                if "B0" in names:
                    bound_scores()
                if previous:
                    rlink = residual(b - 1, b - 1, job(b, "O", kind))
                if keys:
                    take_xT(job(b, "T", kind))
                if previous:
                    row_variance()
                    row_norm(b - 1, rlink)
                if keys:
                    split_queries(b + 2, job(b, "Q", kind))
                if previous:
                    take_yT(job(b, "R0", kind))
                    y_variance()
                    choose(b - 1, rlink, job(b, "R1", kind))
                    y_norm(b - 1, other)
                    place_rows(b - 1, other, rlink, job(b, "R2", kind))

            def prepare(kb, kind, a):
                link = query_stats(kb, kb)
                for j in range(KC):
                    split_keys(kb, j, job(0, f"K{j}{a}", kind), kb == 0, AUX_BANK if kb else EARLY_BANK[f"K{j}"])
                    if j == 0:
                        query_variance()
                query_norm(kb, kb)
                add_bias(kb, kb, link)
                take_xT(job(0, "T" + a, kind))
                split_queries(kb, job(0, "Q" + a, kind), kb == 0)

            prepare(0, "before", "")
            dve.wait_ge(pads_done, 6)
            for j in range(3):
                take_values(0, 0, j, job(0, f"V{j}", "before"), EARLY_BANK[f"V{j}"])
            prepare(1, "first", "a")
            for name in ("x1", "rank", "run", "sides"):
                dve.wait_ge(loaded[name], 16)
            batch(0, 0, 0, "first")
            with dve.Fori(0, B // 2 - 2) as i:
                batch(i * 2 + 1, i, 1, "middle")
                batch(i * 2 + 2, i + 1, 0, "middle")
            batch(B - 3, B // 2 - 2, 1, "middle")
            batch(B - 2, B // 2 - 1, 0, "late")
            nc.vector.tensor_copy(t_pad[:, :], run[0:1, :]).then_inc(pad_ready, 1)
            batch(B - 1, B // 2 - 1, 1, "last")
            copy_out(B - 1)
            dve.wait_ge(o_copied, B + 1)
            olink = spread_sums(B - 1)
            pick(olink, s_pick, o_sum)
            invert(olink)
            pick(olink, o_pick, o_raw)
            divide(job(B, "O", "after"))
            rlink = residual(B - 1, B - 1, job(B, "O", "after"))
            row_variance()
            row_norm(B - 1, rlink)
            take_yT(job(B, "R0", "after"))
            y_variance()
            choose(B - 1, rlink, job(B, "R1", "after"))
            y_norm(B - 1, 1)
            place_rows(B - 1, 1, rlink, job(B, "R2", "after"))

            dve.wait_ge(flag_ready, 1)
            unbounded = dve.value_load(flag[0:1, 0:1], min_val=0, max_val=1)
            with dve.If(unbounded):
                dve.wait_ge(loaded["first"], 16)
                for k in range(2):
                    dve.wait_ge(row_stored[k], (B // 2 + 1) * 16)
                nc.vector.tensor_copy(run[:, :], first_s[:, :]).then_inc(g_reset, 1)
                dve.wait_ge(g_x, 16)
                dve.wait_ge(g_reset, 1)
                with dve.Fori(0, B // 2) as i:
                    for par in range(2):
                        b = i * 2 + par
                        again = i * 2 + (B + par)
                        qlink = query_stats(again, b)
                        dve.wait_ge(g_k_ps, b + 1)
                        nc.vector.tensor_copy(g_kT[:, 0:964].rearrange("d (c m) -> d c m", c=2), ps[:, 0:2, 0:482])\
                            .then_inc(g_k_done, 1)
                        query_variance()
                        nc.vector.tensor_copy(g_kT[:, 964:M], ps[:, 2, 0:480]).then_inc(g_k_done, 1)
                        query_norm(again, b)
                        add_bias(again, b, qlink)
                        take_xT(job(b, "T", "again"))
                        link = Chain(dve, g_chain, b, H + 2)
                        n = job(b, "Q", "again")
                        dve.wait_ge(aux_ps, n + 1)
                        nc.vector.tensor_copy(g_qT, ps[:, AUX_BANK, 0:N]).then_inc(aux_free, 1)
                        dve.wait_ge(aux_free, n + 1)
                        nc.vector.tensor_tensor(g_qbd, g_qT.unsqueeze(1).to_broadcast([D, H, N]),
                                                headmask_s[:, :].unsqueeze(2).to_broadcast([D, H, N]), ALU.mult)\
                            .then_inc(g_qbd_done, 1)
                        dve.wait_ge(g_v_ps, b + 2)
                        nc.vector.tensor_copy(g_v[:, 0:KT - 1, :].rearrange("p t d -> p (t d)"),
                                              ps[:, 4:7, :].rearrange("p c m -> p (c m)")[:, 0:(KT - 1) * D])\
                            .then_inc(g_v_done, 1)
                        nc.vector.tensor_copy(g_v[0:LAST, KT - 1, :], ps[0:LAST, 6, 3 * D:4 * D]).then_inc(g_v_done, 1)
                        for h in range(H):
                            dve.wait_ge(g_s_ps, b * H + h + 1)
                            link(nc.vector.tensor_reduce(smax[:, h:h + 1], ps[0:N, 0:4, 0:M // 4], AX.XY, ALU.max))
                            nc.vector.tensor_scalar(nbias[:, h:h + 1], smax[:, h:h + 1], -SCALE, None, ALU.mult)\
                                .then_inc(g_bias, 1)
                            dve.wait_ge(g_pt_ps, b * H + h + 1)
                            if h:
                                dve.wait_ge(g_o_ps, b * H + h)
                            nc.vector.tensor_copy(g_pT[:, 0:8, :],
                                                  ps[:, 4:6, :].rearrange("p c (t n) -> p (c t) n", t=4)[:, :, 0:N])\
                                .then_inc(g_pt_done, 1)
                            nc.vector.tensor_copy(g_pT[:, 8:11, :],
                                                  ps[:, 6, 0:384].rearrange("p (t n) -> p t n", t=3)[:, :, 0:N])\
                                .then_inc(g_pt_done, 1)
                            nc.vector.tensor_copy(g_pT[0:LAST, 11, :], ps[0:LAST, 6, 384:384 + N]).then_inc(g_pt_done, 1)
                        dve.wait_ge(g_exp, b * H + H)
                        link(nc.vector.reciprocal(sinv, ssum))
                        dve.wait_ge(g_o_ps, b * H + H)
                        nc.vector.tensor_tensor(g_o.rearrange("n (h d) -> n h d", h=H),
                                                ps[0:N, AUX_BANK, 0:D].rearrange("n (h d) -> n h d", h=H),
                                                sinv.unsqueeze(2).to_broadcast([N, H, HD]), ALU.mult).then_inc(g_o_done, 1)
                        dve.wait_ge(g_ot_ps, b + 1)
                        link(nc.vector.tensor_copy(g_oT, ps[:, AUX_BANK, 128:128 + N]))
                        rlink = residual(again, b, job(b, "O", "again"))
                        dve.wait_ge(g_pause, b + 1)
                        nc.vector.memset(credit[0:1, 10:11], 0.0).then_inc(g_pause, 1)
                        row_variance()
                        row_norm(again, rlink)
                        take_yT(job(b, "R0", "again"))
                        y_variance()
                        choose(again, rlink, job(b, "R1", "again"))
                        y_norm(again, par)
                        place_rows(again, par, rlink, job(b, "R2", "again"))
                nc.vector.tensor_copy(t_pad[:, :], run[0:1, :]).then_inc(pad_ready, 1)
                for k in range(2):
                    dve.wait_ge(row_stored[k], (B + 1) * 16)

            for name in ("first", "prefix", "tile_row"):
                dve.wait_ge(loaded[name], 16)
            link = Chain(dve, t_chain, 0, 11)
            link(nc.vector.scalar_tensor_tensor(out=t_int[:, :], in0=run[0:1, :], scalar=float(P - 1), in1=first_s[0:1, :],
                                                op0=ALU.add, op1=ALU.subtract))
            link(nc.vector.tensor_scalar(t_int[:, :], t_int[:, :], P.bit_length() - 1, None, ALU.logical_shift_right))
            link(nc.vector.tensor_copy(t_num[:, :], t_int[:, :]))
            link(nc.vector.tensor_tensor(t_pre[:, :, :], prefix_s[:, :, :],
                                         t_num[:, :].unsqueeze(1).to_broadcast([1, E, E]), ALU.mult))
            link(nc.vector.tensor_reduce(t_cum[:, :], t_pre[:, :, :], AX.X, ALU.add))
            link(nc.vector.tensor_tensor(t_ge[:, :, :], tile_row_s[:, :].unsqueeze(2).to_broadcast([1, TILES, E]),
                                         t_cum[:, :].unsqueeze(1).to_broadcast([1, TILES, E]), ALU.is_ge))
            link(nc.vector.tensor_scalar(t_skip[:, :], t_num[:, :], -float(P), float(REGION), ALU.mult, ALU.add))
            link(nc.vector.tensor_reduce(t_exp[:, :], t_ge[:, :, :], AX.X, ALU.add))
            link(nc.vector.tensor_tensor(t_ge[:, :, :], t_ge[:, :, :],
                                         t_skip[:, :].unsqueeze(1).to_broadcast([1, TILES, E]), ALU.mult))
            link(nc.vector.tensor_reduce(t_row[:, :], t_ge[:, :, :], AX.X, ALU.add))
            link(nc.vector.scalar_tensor_tensor(out=t_row[:, :], in0=tile_row_s[:, :], scalar=float(P), in1=t_row[:, :],
                                                op0=ALU.mult, op1=ALU.add))
            nc.vector.tensor_scalar(table[:, 1, :], t_row[:, :], float(E * REGION), None, ALU.min).then_inc(t_ready, 1)
            nc.vector.tensor_scalar(table[:, 0, :], t_exp[:, :], float(E - 1), None, ALU.min).then_inc(t_ready, 1)
            for k in range(2):
                dve.wait_ge(row_stored[k], (B // 2 + 1) * 16)
            nc.vector.memset(credit[0:1, 11:12], 0.0).then_inc(rows_done, 1)

            def affine(k, j, half):
                dve.wait_ge(f_T_ps, k + 1)
                dve.wait_ge(w_loaded[j], half * 16 + 16)
                nc.vector.tensor_scalar(f_x[j % 2], ps[:, j % 2, 0:P], w_t[j][:, 0:1], w_t[j][:, 1:2],
                                        ALU.mult, ALU.add).then_inc(f_T, 1)

            def finish(k, j, stores):
                expert = dve.value_load(table[0:1, 0, bass.ds(k, 1)], min_val=0, max_val=E - 1)
                dve.wait_ge(f_y_ps, k + 3)
                if stores is not None:
                    dve.wait_ge(out_stored[j % OB], stores * 16)
                nc.vector.tensor_tensor(f_o[j % OB], ps[:, 4 + j % 2, 0:D], b2_s[:, bass.ds(expert, 1), :].squeeze(1),
                                        ALU.add).then_inc(f_half, 1)

            def step(k, j, i, stores):
                affine(k + 2, (j + 2) % TB, i + (j + 2) // TB)
                finish(k, j, stores)

            dve.wait_ge(t_ready, 2)
            dve.wait_ge(loaded["b2"], 16)
            for j in range(2):
                affine(j, j, 0)
            for j in range(TB):
                step(j, j, 0, j // OB if j >= OB else None)
            with dve.Fori(1, TILES // TB - 1) as i:
                for j in range(TB):
                    step(i * TB + j, j, i, i * (TB // OB) + j // OB)
            for k in range(TILES - TB, TILES):
                if k + 2 < TILES:
                    affine(k + 2, (k + 2) % TB, TILES // TB - 1)
                finish(k, k % TB, k // OB)

        @block.tensor
        def _(pe):
            pe.wait_ge(loaded["wk"], 16)

            def keys(j, par, n, bank=AUX_BANK):
                m0, mn = KCH[j]
                if bank == AUX_BANK:
                    pe.wait_ge(aux_free, n)
                nc.tensor.matmul(ps[:, bank, 0:mn], wk_s[:, :], ctx_s[par][:, m0:m0 + mn], start=True, stop=True)\
                    .then_inc(aux_ps, 1)

            def xT(kb, n):
                pe.wait_ge(aux_free, n)
                pe.wait_ge(x_norm, kb + 1)
                nc.tensor.transpose(ps[:, AUX_BANK, 0:N], xn[:, :], ident_s[0:N, 0:N]).then_inc(aux_ps, 1)

            def queries(n):
                pe.wait_ge(aux_free, n)
                nc.tensor.matmul(ps[:, AUX_BANK, 0:N], wq_s[:, :], xnT[:, :], start=True, stop=True).then_inc(aux_ps, 1)

            def values(j, par, n, bank=AUX_BANK):
                if bank == AUX_BANK:
                    pe.wait_ge(aux_free, n)
                for k in range(VCH):
                    t = j * VCH + k
                    mn = min(P, M - t * P)
                    last = nc.tensor.matmul(ps[0:mn, bank, k * D:(k + 1) * D], ctx_s[par][:, t * P:t * P + mn],
                                            wv_s[:, :], start=True, stop=True)
                last.then_inc(aux_ps, 1)

            def output(b, n):
                pe.wait_ge(aux_free, n)
                pe.wait_ge(o_ready, b + 2)
                for c in range(2):
                    last = nc.tensor.matmul(ps[0:N, AUX_BANK, 0:D], o_norm[:, c * N:(c + 1) * N], wox_s[:, c, :],
                                            start=(c == 0), stop=(c == 1))
                last.then_inc(aux_ps, 1)

            def rowsT(b, n):
                pe.wait_ge(aux_free, n)
                pe.wait_ge(r_norm, b + 1)
                nc.tensor.transpose(ps[:, AUX_BANK, 0:N], y_s[:, :], ident_s[0:N, 0:N]).then_inc(aux_ps, 1)

            def logits(n):
                pe.wait_ge(aux_free, n)
                nc.tensor.matmul(ps[0:N, AUX_BANK, 0:E], yT[:, :], cent_s[:, :], start=True, stop=True).then_inc(aux_ps, 1)

            def ranks(b, n):
                pe.wait_ge(aux_free, n)
                pe.wait_ge(r_hot, b + 1)
                nc.tensor.matmul(ps[0:N, AUX_BANK, 0:E], lower_s[:, 0, :], onehot[:, :], start=True, stop=True)
                nc.tensor.matmul(ps[0:N, AUX_BANK, E:2 * E], lower_s[:, 1, :], onehot[:, :], start=True, stop=True)\
                    .then_inc(aux_ps, 1)

            def scores(b, half, par, u, fresh):
                if u == 0:
                    pe.wait_ge(ks_loaded[par], (half + 1) * len(TERMS) * 16)
                    pe.wait_ge(qs_loaded[par], (half + 1) * len(RUNS) * 16)
                if not fresh:
                    pe.wait_ge(exp_done, b * UNITS + u - 1)
                for k in range(UB):
                    t, quad = divmod(UB * u + k, 4)
                    for i in range(2):
                        p = 2 * quad + i
                        last = nc.tensor.matmul(ps[:, UB * (u % 2) + k, i * 2 * N:(i + 1) * 2 * N],
                                                ks[par][:, p, t * P:(t + 1) * P], qs[par][:, p, :],
                                                start=True, stop=True)
                last.then_inc(sc_ps, 1)

            def weigh(b, par, u, alone):
                if alone:
                    pe.wait_ge(exp_done, b * UNITS + u + 1)
                if u == 0:
                    pe.wait_ge(v_part, b + 1)
                    pe.wait_ge(o_copied, b + 1)
                for k in range(UB):
                    t, quad = divmod(UB * u + k, 4)
                    for i in range(2):
                        p = 2 * quad + i
                        q, c = 32 * (p % 4), 2 * N * (p // 4)
                        last = nc.tensor.matmul(ps[q:q + VW, O_BANK, c:c + 2 * N], va[par][:, t, p, :],
                                                probs[u % PSLOTS][:, k, i * 2 * N:(i + 1) * 2 * N],
                                                start=(t == 0 and p < 4), stop=(t == KT - 1 and p >= 4),
                                                skip_group_check=True)
                last.then_inc(pv_done, 1)

            def batch(b, half, par, kind):
                last = kind == "last"
                other, other_half = 1 - par, half + par

                def beside(slot):
                    for name in KINDS[kind]:
                        if (FIRST_SLOT if kind == "first" else SLOT)[name] != slot:
                            continue
                        n = job(b, name, kind)
                        if name == "K0":
                            pe.wait_ge(ctx_loaded[par], (half + 2) * 16)
                        if name == "K0a":
                            pe.wait_ge(ctx_loaded[1], 16)
                        if name[0] == "K":
                            keys(int(name[1]), 1 if name[-1] == "a" else par, n)
                        elif name == "Ta":
                            xT(1, n)
                        elif name == "Qa":
                            queries(n)
                        elif name == "T":
                            xT(b + 2, n)
                        elif name == "Q":
                            queries(n)
                        elif name[0] == "V":
                            values(int(name[1]), other, n)
                        elif name == "B0":
                            pe.wait_ge(b_col, 1)
                            pe.wait_ge(aux_free, n)
                            nc.tensor.matmul(ps[0:B, AUX_BANK, 0:H], bound[:, :], headmask_s[:, :], start=True, stop=True)\
                                .then_inc(aux_ps, 1)
                        elif name == "B1":
                            pe.wait_ge(aux_free, n)
                            nc.tensor.transpose(ps[0:1, AUX_BANK, 0:B], bmax[:, :], ident_s[0:B, 0:B]).then_inc(aux_ps, 1)
                        elif name == "O":
                            output(b - 1, n)
                        elif name == "R0":
                            rowsT(b - 1, n)
                        elif name == "R1":
                            logits(n)
                        else:
                            ranks(b - 1, n)

                for u in range(UNITS):
                    v = u + AHEAD
                    if v < UNITS:
                        scores(b, half, par, v, False)
                    elif not last:
                        scores(b + 1, other_half, other, v - UNITS, False)
                    beside(u)
                    weigh(b, par, u, last and v >= UNITS)
                    beside(u + 0.5)

            pe.wait_ge(ctx_loaded[0], 16)
            for j in range(KC):
                keys(j, 0, job(0, f"K{j}", "before"), EARLY_BANK[f"K{j}"])
            for name in ("ident", "wq", "wv"):
                pe.wait_ge(loaded[name], 16)
            xT(0, job(0, "T", "before"))
            queries(job(0, "Q", "before"))
            for j in range(3):
                values(j, 0, job(0, f"V{j}", "before"), EARLY_BANK[f"V{j}"])
            pe.wait_ge(pads_done, 6)
            pe.wait_ge(consts_ready, 4)
            for name in ("wox", "cent", "lower", "headmask"):
                pe.wait_ge(loaded[name], 16)
            pe.wait_ge(aux_free, len(KINDS["before"]))
            for u in range(AHEAD):
                scores(0, 0, 0, u, True)
            batch(0, 0, 0, "first")
            with pe.Fori(0, B // 2 - 2) as i:
                batch(i * 2 + 1, i, 1, "middle")
                batch(i * 2 + 2, i + 1, 0, "middle")
            batch(B - 3, B // 2 - 2, 1, "middle")
            batch(B - 2, B // 2 - 1, 0, "late")
            batch(B - 1, B // 2 - 1, 1, "last")
            output(B - 1, job(B, "O", "after"))
            rowsT(B - 1, job(B, "R0", "after"))
            logits(job(B, "R1", "after"))
            ranks(B - 1, job(B, "R2", "after"))

            pe.wait_ge(flag_ready, 1)
            unbounded = pe.value_load(flag[0:1, 0:1], min_val=0, max_val=1)
            with pe.If(unbounded):
                pe.wait_ge(loaded["wo"], 16)
                with pe.Fori(0, B // 2) as i:
                    for par in range(2):
                        b = i * 2 + par
                        again = i * 2 + (B + par)
                        pe.wait_ge(g_ctx_loaded, b * 16 + 16)
                        for c, (m0, mn) in enumerate(KCH):
                            last = nc.tensor.matmul(ps[:, c, 0:mn], wk_s[:, :], g_ctx[:, m0:m0 + mn], start=True, stop=True)
                        last.then_inc(g_k_ps, 1)
                        for t in range(KT):
                            mn = min(P, M - t * P)
                            last = nc.tensor.matmul(ps[0:mn, 4 + t // 4, (t % 4) * D:(t % 4 + 1) * D],
                                                    g_ctx[:, t * P:t * P + mn], wv_s[:, :], start=True, stop=True)
                        last.then_inc(g_v_ps, 1)
                        xT(again, job(b, "T", "again"))
                        queries(job(b, "Q", "again"))
                        pe.wait_ge(g_k_done, b * 2 + 2)
                        pe.wait_ge(g_v_done, b * 2 + 2)
                        pe.wait_ge(g_qbd_done, b + 1)
                        for h in range(H):
                            if h:
                                pe.wait_ge(g_exp, b * H + h)
                            for c in range(4):
                                last = nc.tensor.matmul(ps[0:N, c, 0:M // 4], g_qbd[:, h, :],
                                                        g_kT[:, c * (M // 4):(c + 1) * (M // 4)], start=True, stop=True)
                            last.then_inc(g_s_ps, 1)
                            pe.wait_ge(g_exp, b * H + h + 1)
                            for t in range(KT):
                                mn = min(P, M - t * P)
                                last = nc.tensor.transpose(ps[0:mn, 4 + t // 4, (t % 4) * D:(t % 4) * D + N],
                                                           g_p[:, t * P:t * P + mn], ident_s[0:N, 0:N])
                            last.then_inc(g_pt_ps, 1)
                            pe.wait_ge(g_pt_done, (b * H + h + 1) * 3)
                            for t in range(KT):
                                mn = min(P, M - t * P)
                                last = nc.tensor.matmul(ps[0:N, AUX_BANK, h * HD:(h + 1) * HD], g_pT[0:mn, t, :],
                                                        g_v[0:mn, t, h * HD:(h + 1) * HD], start=(t == 0),
                                                        stop=(t == KT - 1))
                            last.then_inc(g_o_ps, 1)
                        pe.wait_ge(g_o_done, b + 1)
                        nc.tensor.transpose(ps[:, AUX_BANK, 128:128 + N], g_o, ident_s[0:N, 0:N]).then_inc(g_ot_ps, 1)
                        pe.wait_ge(g_chain, b * (H + 2) + H + 2)
                        n = job(b, "O", "again")
                        pe.wait_ge(aux_free, n)
                        nc.tensor.matmul(ps[0:N, AUX_BANK, 0:D], g_oT, wo_s[:, :], start=True, stop=True).then_inc(aux_ps, 1)
                        rowsT(again, job(b, "R0", "again"))
                        logits(job(b, "R1", "again"))
                        ranks(again, job(b, "R2", "again"))

            def turn(k, j, half):
                pe.wait_ge(y_loaded[j], half * 16 + 16)
                nc.tensor.transpose(ps[:, j % 2, 0:P], y_t[j][:, 0:D], ident_s[:, :]).then_inc(f_T_ps, 1)

            def expert_of(k):
                return pe.value_load(table[0:1, 0, bass.ds(k, 1)], min_val=0, max_val=E - 1)

            def hidden(k, j):
                pe.wait_ge(f_T, k + 1)
                w = w_t[j][:, 2 + FC:PACK]
                for c in range(FC):
                    ins = nc.tensor.matmul(ps[:, HIDDEN[j % 2] + c // 2, (c % 2) * P:(c % 2 + 1) * P],
                                           w[:, c * P:(c + 1) * P], f_x[j % 2], start=True, stop=True)
                    if c % 2:
                        ins.then_inc(f_h_ps, 1)

            def result(k, j, expert):
                o = ps[:, 4 + j % 2, 0:D]
                w = w2_s[:, bass.ds(expert, 1), :].squeeze(1)
                if not isinstance(k, int) or k >= 2:
                    pe.wait_ge(f_half, k - 1)
                for c in range(FC):
                    pe.wait_ge(f_hid, k * FC + c + 1)
                    last = nc.tensor.matmul(o, f_h[j % 2][:, c, :], w[:, c * D:(c + 1) * D], start=(c == 0),
                                            stop=(c == FC - 1))
                last.then_inc(f_y_ps, 1)

            def step(k, j, half):
                hidden(k + 1, (j + 1) % TB)
                turn(k + 2, (j + 2) % TB, half + (j + 2) // TB)
                result(k, j, expert_of(k))

            pe.wait_ge(t_ready, 2)
            pe.wait_ge(loaded["w2"], 16)
            turn(0, 0, 0)
            hidden(0, 0)
            turn(1, 1, 0)
            for j in range(TB):
                step(j, j, 0)
            with pe.Fori(1, TILES // TB - 1) as i:
                for j in range(TB):
                    step(i * TB + j, j, i)
            for k in range(TILES - TB, TILES - 2):
                step(k, k % TB, TILES // TB - 1)
            hidden(TILES - 1, TB - 1)
            result(TILES - 2, TB - 2, expert_of(TILES - 2))
            result(TILES - 1, TB - 1, expert_of(TILES - 1))


def kernel(x, ctx_1024, L0_xattn_wq, L0_xattn_wk, L0_xattn_wv, L0_xattn_wo, L0_xattn_bo, L0_ffn_centroids,
           L0_ffn_ln_g, L0_ffn_ln_b, L0_ffn_W1, L0_ffn_b1, L0_ffn_W2, L0_ffn_b2):
    import numpy as np
    import concourse.bacc as bacc
    from concourse.bass_utils import run_bass_kernel_spmd

    def lay(a):
        return np.ascontiguousarray(np.asarray(a))

    woT = lay(np.asarray(L0_xattn_wo).T)
    wox = np.zeros((4, 32, 2, D), np.float32)
    wox[:, 0:2 * HD] = woT.reshape(2, 4, 2 * HD, D).transpose(1, 2, 0, 3)
    second = (np.arange(P) % 32 // HD == 1).astype(np.float32)
    pack = np.zeros((E, P, PACK), np.float32)
    pack[:, :, 0] = np.asarray(L0_ffn_ln_g)
    pack[:, :, 1] = np.asarray(L0_ffn_ln_b)
    pack[:, :, 2 + FC:] = np.asarray(L0_ffn_W1)
    pack[:, :, 2:2 + FC] = np.asarray(L0_ffn_b1).reshape(E, FC, P).transpose(0, 2, 1)
    pad_row = np.zeros((P, ROW), np.float32)
    pad_row[:, 2 * D:].view(np.int32)[:] = 1 << 20
    before = np.arange(N)
    arrays = {
        "x": lay(x),
        "ctxT": lay(np.asarray(ctx_1024).transpose(0, 2, 1)),
        "wqT": lay(np.asarray(L0_xattn_wq).T), "wkT": lay(np.asarray(L0_xattn_wk).T),
        "wvT": lay(np.asarray(L0_xattn_wv).T), "woT": woT, "wox": wox.reshape(P, 2, D),
        "sides": np.stack([1 - second, second], 1),
        "bo": lay(np.broadcast_to(np.asarray(L0_xattn_bo), (N, D))),
        "centT": lay(np.asarray(L0_ffn_centroids).T),
        "pack": pack,
        "w2": lay(np.asarray(L0_ffn_W2).reshape(E, FC, P, D).transpose(2, 0, 1, 3).reshape(P, E, FC * D)),
        "b2": lay(np.broadcast_to(np.asarray(L0_ffn_b2), (P, E, D))),
        "ident": np.eye(P, dtype=np.float32),
        "rank": np.broadcast_to(np.arange(E, 0, -1, dtype=np.float32), (N, E)).copy(),
        "headmask": np.kron(np.eye(H, dtype=np.float32), np.ones((HD, 1), np.float32)),
        "lower": np.stack([(before[:, None] < before[None, :]), np.ones((N, N), bool)], 1).astype(np.float32),
        "ids": (np.arange(B, dtype=np.int32)[None, :] * N + np.arange(N, dtype=np.int32)[:, None]),
        "first_row": np.broadcast_to(np.arange(E, dtype=np.float32) * REGION, (N, E)).copy(),
        "prefix": (np.arange(E)[:, None] >= np.arange(E)[None, :]).astype(np.float32)[None],
        "tile_row": np.arange(TILES, dtype=np.float32)[None],
        "pad_row": pad_row,
    }
    nc = bacc.Bacc("TRN2", target_bir_lowering=False, num_devices=1)
    ins = [nc.dram_tensor(f"in_{n}", a.shape, mybir.dt.from_np(a.dtype), kind="ExternalInput").ap()
           for n, a in arrays.items()]
    out = nc.dram_tensor("out_x", (B, N, D), F32, kind="ExternalOutput").ap()
    build(nc, *ins, out)
    r = run_bass_kernel_spmd(nc, [{f"in_{n}": a for n, a in arrays.items()}], core_ids=[0])
    return r.results[0]["out_x"]
```
